# Optimizing a Trainium2 kernel written in Bass

```python
import numpy as np
import jax
import jax.numpy as jnp

def _softmax(x, axis=-1):
    return jax.nn.softmax(x, axis=axis)

def _gelu(x):
    return jax.nn.gelu(x, approximate=True)

def _silu(x):
    return jax.nn.silu(x)

def _sigmoid(x):
    return jax.nn.sigmoid(x)

def _layernorm(x, axis=-1, eps=1e-05):
    m = jnp.mean(x, axis=axis, keepdims=True)
    v = jnp.var(x, axis=axis, keepdims=True)
    return (x - m) / jnp.sqrt(v + eps)

def _scatter_add(tgt, idx, src, axis=0):
    return tgt.at[idx].add(src)

def _segment_sum(src, seg, n):
    return jax.ops.segment_sum(src, seg, n)
kernel_name = 'mk_seq_preln_d2_jaxref_r8_b128a2'

def setup_inputs(seed: int=0):
    np.random.seed(seed)
    _w = jnp.asarray

    def _L0_attn_setup():
        import jax, jax.numpy as jnp
        import numpy as np
        D_MODEL = 128
        N_HEADS = 16
        D_HEAD = D_MODEL // N_HEADS

        def _rmsnorm(x, w):
            xf = x.astype(jnp.float32)
            rms = jnp.mean(xf * xf, axis=-1, keepdims=True)
            return (xf / jnp.sqrt(rms + 1e-06) * w.astype(jnp.float32)).astype(x.dtype)
        key = jax.random.key(seed)
        ks = jax.random.split(key, 7)
        x = jax.random.normal(ks[0], (1, 512, D_MODEL), dtype=jnp.float32)
        Wqkv = jax.random.normal(ks[1], (3 * D_MODEL, D_MODEL), dtype=jnp.float32) * (1.0 / np.sqrt(D_MODEL))
        bqkv = jax.random.normal(ks[2], (3 * D_MODEL,), dtype=jnp.float32) * 0.01
        Wo = jax.random.normal(ks[3], (D_MODEL, D_MODEL), dtype=jnp.float32) * (1.0 / np.sqrt(D_MODEL))
        bo = jax.random.normal(ks[4], (D_MODEL,), dtype=jnp.float32) * 0.01
        wq = jnp.ones((D_HEAD,), dtype=jnp.float32)
        wk = jnp.ones((D_HEAD,), dtype=jnp.float32)
        return {'x': x, 'Wqkv': Wqkv, 'bqkv': bqkv, 'Wo': Wo, 'bo': bo, 'wq': wq, 'wk': wk}
    _L0_attn_in = _L0_attn_setup()

    def _L0_ffn_setup():
        import jax, jax.numpy as jnp
        import numpy as np
        DIM = 128
        DEPTH = 6
        HEADS = 16
        DIM_HEAD = 64
        WINDOW = 32
        INNER = HEADS * DIM_HEAD
        DIM_INNER = int(DIM * 4 * 2 / 3)
        QK_SCALE = 8.0

        def shift_tokens(t):
            a, s = jnp.split(t, 2, -1)
            s = jnp.pad(s, ((0, 0), (1, 0), (0, 0)))[:, :-1]
            return jnp.concatenate([a, s], -1)

        def l2norm(t):
            return t / jnp.maximum(jnp.linalg.norm(t, axis=-1, keepdims=True), 1e-12)

        def rotate_half(x):
            x1, x2 = jnp.split(x, 2, -1)
            return jnp.concatenate([-x2, x1], -1)

        def rotary_tables(n):
            half = jnp.arange(0, DIM_HEAD, 2, dtype=jnp.float32)
            inv_freq = 1.0 / 10000.0 ** (half / DIM_HEAD)
            t = jnp.arange(n, dtype=jnp.float32)
            freqs = t[:, None] * inv_freq[None, :]
            freqs = jnp.concatenate([freqs, freqs], -1)
            base_scale = (half + 0.4 * DIM_HEAD) / (1.4 * DIM_HEAD)
            power = (t - n // 2) / (WINDOW // 2)
            scale = base_scale[None, :] ** power[:, None]
            scale = jnp.concatenate([scale, scale], -1)
            return (freqs, scale)

        def local_attention(q, k, v):
            b, h, n, d = q.shape
            w = WINDOW
            nw = n // w
            bq = q.reshape(b, h, nw, w, d)
            bk = k.reshape(b, h, nw, w, d)
            bv = v.reshape(b, h, nw, w, d)

            def look(t):
                p = jnp.pad(t, ((0, 0), (0, 0), (1, 0), (0, 0), (0, 0)))
                return jnp.concatenate([p[:, :, :nw], p[:, :, 1:]], axis=3)
            bk2, bv2 = (look(bk), look(bv))
            seq = jnp.arange(n).reshape(nw, w)
            seq_p = jnp.pad(seq, ((1, 0), (0, 0)), constant_values=-1)
            jt = jnp.concatenate([seq_p[:nw], seq_p[1:]], axis=1)
            it = seq[:, :, None]
            jb = jt[:, None, :]
            mask = (it < jb) | (it > jb + w) | (jb == -1)
            sim = jnp.einsum('bhwie,bhwje->bhwij', bq, bk2) * QK_SCALE
            sim = jnp.where(mask, -jnp.finfo(sim.dtype).max, sim)
            attn = jax.nn.softmax(sim, -1)
            out = jnp.einsum('bhwij,bhwje->bhwie', attn, bv2)
            return out.reshape(b, h, n, d)

        def attn_layer(x, Wqkv, qs, ksc, Wo):
            b, n, _ = x.shape
            qkv = x @ Wqkv
            q, k, v = jnp.split(qkv, 3, -1)
            sh = lambda t: t.reshape(b, n, HEADS, DIM_HEAD).transpose(0, 2, 1, 3)
            q, k, v = (sh(q), sh(k), sh(v))
            q = l2norm(q) * qs
            k = l2norm(k) * ksc
            freqs, scale = rotary_tables(n)
            cos, sin = (jnp.cos(freqs), jnp.sin(freqs))
            q = q * cos * scale + rotate_half(q) * sin * scale
            inv = 1.0 / scale
            k = k * cos * inv + rotate_half(k) * sin * inv
            out = local_attention(q, k, v)
            out = out.transpose(0, 2, 1, 3).reshape(b, n, INNER)
            return out @ Wo

        def ffn_layer(x, g, bln, W1, b1, W2, b2):
            mu = x.mean(-1, keepdims=True)
            var = ((x - mu) ** 2).mean(-1, keepdims=True)
            xn = (x - mu) / jnp.sqrt(var + 1e-05) * g + bln
            hg = xn @ W1 + b1
            a, gate = jnp.split(hg, 2, -1)
            return a * jax.nn.gelu(gate, approximate=False) @ W2 + b2
        key = jax.random.key(seed)
        ks = jax.random.split(key, 8)
        B, N = (2, 256)
        init = lambda k, shape: jax.random.normal(k, shape, jnp.float32) * 0.02
        return {'x': jax.random.normal(ks[0], (B, N, DIM), jnp.float32), 'Wqkv': init(ks[1], (DEPTH, DIM, 3 * INNER)), 'q_scale': jnp.ones((DEPTH, DIM_HEAD), jnp.float32), 'k_scale': jnp.ones((DEPTH, DIM_HEAD), jnp.float32), 'Wo': init(ks[2], (DEPTH, INNER, DIM)), 'ln_g': jnp.ones((DEPTH, DIM), jnp.float32), 'ln_b': jnp.zeros((DEPTH, DIM), jnp.float32), 'W1': init(ks[3], (DEPTH, DIM, 2 * DIM_INNER)), 'b1': jnp.zeros((DEPTH, 2 * DIM_INNER), jnp.float32), 'W2': init(ks[4], (DEPTH, DIM_INNER, DIM)), 'b2': jnp.zeros((DEPTH, DIM), jnp.float32)}
    _L0_ffn_in = _L0_ffn_setup()

    def _L1_attn_setup():
        import jax, jax.numpy as jnp
        import numpy as np
        N_EMBD = 128
        N_HEAD = 16
        HEAD_DIM = N_EMBD // N_HEAD
        LATENT_DIM = N_EMBD // 2
        B, T = (4, 256)
        key = jax.random.key(seed)
        ks = jax.random.split(key, 5)

        def init(k, fan_in, fan_out):
            bound = 1.0 / np.sqrt(fan_in)
            return jax.random.uniform(k, (fan_in, fan_out), jnp.float32, -bound, bound)
        return {'x': jax.random.normal(ks[0], (B, T, N_EMBD), jnp.float32), 'Wc_down': init(ks[1], N_EMBD, LATENT_DIM), 'Wq_up': init(ks[2], LATENT_DIM, N_EMBD), 'Wkv_up': init(ks[3], LATENT_DIM, 2 * HEAD_DIM), 'Wc_proj': init(ks[4], N_EMBD, N_EMBD)}
    _L1_attn_in = _L1_attn_setup()

    def _L1_ffn_setup():
        import jax, jax.numpy as jnp
        import numpy as np
        BLOCK = 16
        _GRID = jnp.array([0.0, 0.5, 1.0, 1.5, 2.0, 3.0, 4.0, 6.0], dtype=jnp.float32)
        _MID = jnp.array([0.25, 0.75, 1.25, 1.75, 2.5, 3.5, 5.0], dtype=jnp.float32)

        def fp4_quant_dequant(x):
            shape = x.shape
            xb = x.reshape(shape[:-1] + (shape[-1] // BLOCK, BLOCK))
            scale = jnp.max(jnp.abs(xb), axis=-1, keepdims=True) / 6.0
            scale = jnp.maximum(scale, jnp.float32(1e-12))
            xn = xb / scale
            idx = jnp.searchsorted(_MID, jnp.abs(xn))
            q = _GRID[idx] * jnp.sign(xn) * scale
            return q.reshape(shape)

        def fp4_linear(x, w):
            xq = fp4_quant_dequant(x)
            wq = fp4_quant_dequant(w)
            return jnp.einsum('bsk,nk->bsn', xq, wq)
        key = jax.random.key(seed)
        k1, k2, k3, k4 = jax.random.split(key, 4)
        H, I = (128, 352)
        x = jax.random.normal(k1, (4, 512, H), dtype=jnp.float32)
        w_gate = jax.random.normal(k2, (I, H), dtype=jnp.float32) * 0.02
        w_up = jax.random.normal(k3, (I, H), dtype=jnp.float32) * 0.02
        w_down = jax.random.normal(k4, (H, I), dtype=jnp.float32) * 0.02
        return {'x': x, 'w_gate': w_gate, 'w_up': w_up, 'w_down': w_down}
    _L1_ffn_in = _L1_ffn_setup()
    _d = {'L0_attn_x': _L0_attn_in['x'], 'L0_attn_Wqkv': _L0_attn_in['Wqkv'], 'L0_attn_bqkv': _L0_attn_in['bqkv'], 'L0_attn_Wo': _L0_attn_in['Wo'], 'L0_attn_bo': _L0_attn_in['bo'], 'L0_attn_wq': _L0_attn_in['wq'], 'L0_attn_wk': _L0_attn_in['wk'], 'L0_ffn_Wqkv': _L0_ffn_in['Wqkv'], 'L0_ffn_q_scale': _L0_ffn_in['q_scale'], 'L0_ffn_k_scale': _L0_ffn_in['k_scale'], 'L0_ffn_Wo': _L0_ffn_in['Wo'], 'L0_ffn_ln_g': _L0_ffn_in['ln_g'], 'L0_ffn_ln_b': _L0_ffn_in['ln_b'], 'L0_ffn_W1': _L0_ffn_in['W1'], 'L0_ffn_b1': _L0_ffn_in['b1'], 'L0_ffn_W2': _L0_ffn_in['W2'], 'L0_ffn_b2': _L0_ffn_in['b2'], 'L1_attn_Wc_down': _L1_attn_in['Wc_down'], 'L1_attn_Wq_up': _L1_attn_in['Wq_up'], 'L1_attn_Wkv_up': _L1_attn_in['Wkv_up'], 'L1_attn_Wc_proj': _L1_attn_in['Wc_proj'], 'L1_ffn_w_gate': _L1_ffn_in['w_gate'], 'L1_ffn_w_up': _L1_ffn_in['w_up'], 'L1_ffn_w_down': _L1_ffn_in['w_down']}
    _x0 = _d['L0_attn_x']
    _d['L0_attn_x'] = jax.random.normal(jax.random.fold_in(jax.random.key(seed), 1), (4, 1024, 128), dtype=_x0.dtype)
    del _x0
    return _d

def reference(L0_attn_x, L0_attn_Wqkv, L0_attn_bqkv, L0_attn_Wo, L0_attn_bo, L0_attn_wq, L0_attn_wk, L0_ffn_Wqkv, L0_ffn_q_scale, L0_ffn_k_scale, L0_ffn_Wo, L0_ffn_ln_g, L0_ffn_ln_b, L0_ffn_W1, L0_ffn_b1, L0_ffn_W2, L0_ffn_b2, L1_attn_Wc_down, L1_attn_Wq_up, L1_attn_Wkv_up, L1_attn_Wc_proj, L1_ffn_w_gate, L1_ffn_w_up, L1_ffn_w_down):

    def _L0_attn_ref(x, Wqkv, bqkv, Wo, bo, wq, wk):
        import jax, jax.numpy as jnp
        import numpy as np
        D_MODEL = 128
        N_HEADS = 16
        D_HEAD = D_MODEL // N_HEADS

        def _rmsnorm(x, w):
            xf = x.astype(jnp.float32)
            rms = jnp.mean(xf * xf, axis=-1, keepdims=True)
            return (xf / jnp.sqrt(rms + 1e-06) * w.astype(jnp.float32)).astype(x.dtype)
        b, s, d = x.shape
        qkv = x @ Wqkv.T + bqkv
        q, k, v = jnp.split(qkv, 3, axis=-1)
        q = q.reshape(b, s, N_HEADS, D_HEAD)
        k = k.reshape(b, s, N_HEADS, D_HEAD)
        v = v.reshape(b, s, N_HEADS, D_HEAD)
        q = _rmsnorm(q, wq)
        k = _rmsnorm(k, wk)
        qf = q.astype(jnp.float32)
        kf = k.astype(jnp.float32)
        vf = v.astype(jnp.float32)
        attn = jnp.einsum('bqhd,bkhd->bhqk', qf, kf)
        attn = jax.nn.softmax(attn, axis=-1)
        z = jnp.einsum('bhqk,bkhd->bqhd', attn, vf).astype(x.dtype)
        z = z.reshape(b, s, d)
        return z @ Wo.T + bo

    def _L0_ffn_ref(x, Wqkv, q_scale, k_scale, Wo, ln_g, ln_b, W1, b1, W2, b2):
        import jax, jax.numpy as jnp
        import numpy as np
        DIM = 128
        DEPTH = 6
        HEADS = 16
        DIM_HEAD = 64
        WINDOW = 32
        INNER = HEADS * DIM_HEAD
        DIM_INNER = int(DIM * 4 * 2 / 3)
        QK_SCALE = 8.0

        def shift_tokens(t):
            a, s = jnp.split(t, 2, -1)
            s = jnp.pad(s, ((0, 0), (1, 0), (0, 0)))[:, :-1]
            return jnp.concatenate([a, s], -1)

        def l2norm(t):
            return t / jnp.maximum(jnp.linalg.norm(t, axis=-1, keepdims=True), 1e-12)

        def rotate_half(x):
            x1, x2 = jnp.split(x, 2, -1)
            return jnp.concatenate([-x2, x1], -1)

        def rotary_tables(n):
            half = jnp.arange(0, DIM_HEAD, 2, dtype=jnp.float32)
            inv_freq = 1.0 / 10000.0 ** (half / DIM_HEAD)
            t = jnp.arange(n, dtype=jnp.float32)
            freqs = t[:, None] * inv_freq[None, :]
            freqs = jnp.concatenate([freqs, freqs], -1)
            base_scale = (half + 0.4 * DIM_HEAD) / (1.4 * DIM_HEAD)
            power = (t - n // 2) / (WINDOW // 2)
            scale = base_scale[None, :] ** power[:, None]
            scale = jnp.concatenate([scale, scale], -1)
            return (freqs, scale)

        def local_attention(q, k, v):
            b, h, n, d = q.shape
            w = WINDOW
            nw = n // w
            bq = q.reshape(b, h, nw, w, d)
            bk = k.reshape(b, h, nw, w, d)
            bv = v.reshape(b, h, nw, w, d)

            def look(t):
                p = jnp.pad(t, ((0, 0), (0, 0), (1, 0), (0, 0), (0, 0)))
                return jnp.concatenate([p[:, :, :nw], p[:, :, 1:]], axis=3)
            bk2, bv2 = (look(bk), look(bv))
            seq = jnp.arange(n).reshape(nw, w)
            seq_p = jnp.pad(seq, ((1, 0), (0, 0)), constant_values=-1)
            jt = jnp.concatenate([seq_p[:nw], seq_p[1:]], axis=1)
            it = seq[:, :, None]
            jb = jt[:, None, :]
            mask = (it < jb) | (it > jb + w) | (jb == -1)
            sim = jnp.einsum('bhwie,bhwje->bhwij', bq, bk2) * QK_SCALE
            sim = jnp.where(mask, -jnp.finfo(sim.dtype).max, sim)
            attn = jax.nn.softmax(sim, -1)
            out = jnp.einsum('bhwij,bhwje->bhwie', attn, bv2)
            return out.reshape(b, h, n, d)

        def attn_layer(x, Wqkv, qs, ksc, Wo):
            b, n, _ = x.shape
            qkv = x @ Wqkv
            q, k, v = jnp.split(qkv, 3, -1)
            sh = lambda t: t.reshape(b, n, HEADS, DIM_HEAD).transpose(0, 2, 1, 3)
            q, k, v = (sh(q), sh(k), sh(v))
            q = l2norm(q) * qs
            k = l2norm(k) * ksc
            freqs, scale = rotary_tables(n)
            cos, sin = (jnp.cos(freqs), jnp.sin(freqs))
            q = q * cos * scale + rotate_half(q) * sin * scale
            inv = 1.0 / scale
            k = k * cos * inv + rotate_half(k) * sin * inv
            out = local_attention(q, k, v)
            out = out.transpose(0, 2, 1, 3).reshape(b, n, INNER)
            return out @ Wo

        def ffn_layer(x, g, bln, W1, b1, W2, b2):
            mu = x.mean(-1, keepdims=True)
            var = ((x - mu) ** 2).mean(-1, keepdims=True)
            xn = (x - mu) / jnp.sqrt(var + 1e-05) * g + bln
            hg = xn @ W1 + b1
            a, gate = jnp.split(hg, 2, -1)
            return a * jax.nn.gelu(gate, approximate=False) @ W2 + b2
        for i in range(DEPTH):
            x = attn_layer(shift_tokens(x), Wqkv[i], q_scale[i], k_scale[i], Wo[i]) + x
            x = ffn_layer(shift_tokens(x), ln_g[i], ln_b[i], W1[i], b1[i], W2[i], b2[i]) + x
        return x

    def _L1_attn_ref(x, Wc_down, Wq_up, Wkv_up, Wc_proj):
        import jax, jax.numpy as jnp
        import numpy as np
        N_EMBD = 128
        N_HEAD = 16
        HEAD_DIM = N_EMBD // N_HEAD
        LATENT_DIM = N_EMBD // 2
        B, T = (4, 256)
        Bsz, Tlen, C = x.shape
        latent = x @ Wc_down
        q = (latent @ Wq_up).reshape(Bsz, Tlen, N_HEAD, HEAD_DIM)
        kv = latent @ Wkv_up
        k, v = (kv[..., :HEAD_DIM], kv[..., HEAD_DIM:])
        scale = 1.0 / np.sqrt(HEAD_DIM)
        att = jnp.einsum('bthd,bsd->bhts', q, k) * scale
        causal = jnp.tril(jnp.ones((Tlen, Tlen), dtype=bool))
        att = jnp.where(causal[None, None], att, -jnp.inf)
        att = jax.nn.softmax(att, axis=-1)
        y = jnp.einsum('bhts,bsd->bthd', att, v).reshape(Bsz, Tlen, C)
        return y @ Wc_proj

    def _L1_ffn_ref(x, w_gate, w_up, w_down):
        import jax, jax.numpy as jnp
        import numpy as np
        BLOCK = 16
        _GRID = jnp.array([0.0, 0.5, 1.0, 1.5, 2.0, 3.0, 4.0, 6.0], dtype=jnp.float32)
        _MID = jnp.array([0.25, 0.75, 1.25, 1.75, 2.5, 3.5, 5.0], dtype=jnp.float32)

        def fp4_quant_dequant(x):
            shape = x.shape
            xb = x.reshape(shape[:-1] + (shape[-1] // BLOCK, BLOCK))
            scale = jnp.max(jnp.abs(xb), axis=-1, keepdims=True) / 6.0
            scale = jnp.maximum(scale, jnp.float32(1e-12))
            xn = xb / scale
            idx = jnp.searchsorted(_MID, jnp.abs(xn))
            q = _GRID[idx] * jnp.sign(xn) * scale
            return q.reshape(shape)

        def fp4_linear(x, w):
            xq = fp4_quant_dequant(x)
            wq = fp4_quant_dequant(w)
            return jnp.einsum('bsk,nk->bsn', xq, wq)
        gate = fp4_linear(x, w_gate)
        y = fp4_linear(x, w_up)
        h = jax.nn.silu(gate) * y
        return fp4_linear(h, w_down)
    x = L0_attn_x
    x = x + _L0_attn_ref(_layernorm(x, axis=-1), L0_attn_Wqkv, L0_attn_bqkv, L0_attn_Wo, L0_attn_bo, L0_attn_wq, L0_attn_wk)
    x = x + _L0_ffn_ref(_layernorm(x, axis=-1), L0_ffn_Wqkv, L0_ffn_q_scale, L0_ffn_k_scale, L0_ffn_Wo, L0_ffn_ln_g, L0_ffn_ln_b, L0_ffn_W1, L0_ffn_b1, L0_ffn_W2, L0_ffn_b2)
    x = x + _L1_attn_ref(_layernorm(x, axis=-1), L1_attn_Wc_down, L1_attn_Wq_up, L1_attn_Wkv_up, L1_attn_Wc_proj)
    x = x + _L1_ffn_ref(_layernorm(x, axis=-1), L1_ffn_w_gate, L1_ffn_w_up, L1_ffn_w_down)
    return x

_drawn_inputs = setup_inputs


def setup_inputs(seed=0):
    import zlib

    import numpy as np

    out = dict(_drawn_inputs(seed))
    spreads = {'L0_attn_wq': (1.0, 0.2),
     'L0_attn_wk': (1.0, 0.2),
     'L0_ffn_q_scale': (1.0, 0.6),
     'L0_ffn_k_scale': (1.0, 0.6),
     'L0_ffn_ln_g': (1.0, 0.6),
     'L0_ffn_ln_b': (0.0, 0.8),
     'L0_ffn_b1': (0.0, 0.8),
     'L0_ffn_b2': (0.0, 0.1)}
    factors = {'L0_attn_bqkv': 4.725,
     'L0_attn_bo': 5.635,
     'L0_ffn_W1': 3.68,
     'L0_ffn_W2': 3.615,
     'L1_attn_Wc_down': 3.327,
     'L1_attn_Wq_up': 8.0,
     'L1_attn_Wkv_up': 3.617,
     'L1_attn_Wc_proj': 3.391,
     'L1_ffn_w_gate': 8.0,
     'L1_ffn_w_up': 8.0,
     'L1_ffn_w_down': 8.0}
    for name, (base, spread) in spreads.items():
        noise = np.random.default_rng([zlib.crc32(name.encode()), seed]).standard_normal(out[name].shape)
        drawn = base * np.exp(spread * noise) if base else spread * noise
        out[name] = jnp.asarray(drawn.astype(out[name].dtype))
    for name, factor in factors.items():
        out[name] = (out[name] * factor).astype(out[name].dtype)
    return out
```

```python
import numpy as np
import concourse.bass as bass
from concourse import mybir
from contextlib import ExitStack

F32 = mybir.dt.float32
BF16 = mybir.dt.bfloat16
ALU = mybir.AluOpType
ACT = mybir.ActivationFunctionType
AX = mybir.AxisListType
ds = bass.ds

P = 128
BATCH, SEQ = 4, 1024
TOK = BATCH * SEQ
CH = 512
NCH = TOK // CH
PAIRS = NCH // 2
HEADS, HD = 16, 8
GRP = 4
NGRP = HEADS // GRP
QT = SEQ // P
PARTS = 3
STACK = PARTS * PARTS * HD
KROWS = 96
NEG = -1.0e30
LN_EPS, RMS_EPS = 1e-5, 1e-6


def alloc(ctx, nc, tag):
    taken = []

    def sb(name, shape, dt=F32):
        return ctx.enter_context(nc.sbuf_tensor(f"{tag}_{name}", shape, dt))

    def ps(name, shape, dt=F32):
        return ctx.enter_context(nc.psum_tensor(f"{tag}_{name}", shape, dt))

    def sem(name):
        taken.append(nc.alloc_semaphore(f"{tag}_{name}"))
        return taken[-1]

    def clear():
        nc.clear_and_free_semaphores(taken)
        nc.all_engine_barrier()

    ctx.callback(clear)

    def sem2(name):
        return [sem(f"{name}{u}") for u in range(2)]

    return sb, ps, sem, sem2


def bcast_mid(ap, n):
    return ap.unsqueeze(1).to_broadcast([ap.shape[0], n, ap.shape[1]])


def bcast_last(ap, n):
    return ap.unsqueeze(2).to_broadcast([ap.shape[0], ap.shape[1], n])


def load_residual(nc, d, XR, ident, ones, ones_mean):
    with ExitStack() as ctx:
        sb, ps, sem, sem2 = alloc(ctx, nc, "in")
        x_loaded, consts_loaded = sem("x_loaded"), sem("consts_loaded")
        block = ctx.enter_context(nc.Block())

        @block.sync
        def _(sp):
            for b in range(BATCH):
                sp.dma_start(XR[:, b * SEQ:(b + 1) * SEQ], d["x_t"][:, b * SEQ:(b + 1) * SEQ]).then_inc(x_loaded, 16)
            sp.dma_start(ident[:, :], d["c_ident"]).then_inc(consts_loaded, 16)
            sp.dma_start(ones_mean[:, :], d["c_ones_mean"]).then_inc(consts_loaded, 16)
            sp.dma_start(ones[:, :], d["c_ones"]).then_inc(consts_loaded, 16)
            sp.wait_ge(x_loaded, 16 * BATCH)
            sp.wait_ge(consts_loaded, 48)


def store_residual(nc, out_t, XR):
    with ExitStack() as ctx:
        sb, ps, sem, sem2 = alloc(ctx, nc, "out")
        out_stored = sem("out_stored")
        block = ctx.enter_context(nc.Block())

        @block.sync
        def _(sp):
            for b in range(BATCH):
                sp.dma_start(out_t[:, b * SEQ:(b + 1) * SEQ], XR[:, b * SEQ:(b + 1) * SEQ]).then_inc(out_stored, 16)
            sp.wait_ge(out_stored, 16 * BATCH)


def project_heads(nc, tag, XR, ident, ones, ones_mean, w, q_parts, k_parts, v_rows):
    rms = "wq" in w
    KF = P if rms else HD
    LAT = 64
    with ExitStack() as ctx:
        sb, ps, sem, sem2 = alloc(ctx, nc, tag)
        cen = sb("cen", [P, 2, CH])
        sq = sb("sq", [P, 2, CH])
        ve = sb("ve", [P, 2, CH // P])
        rs = sb("rs", [P, 2, CH // P])
        rs_diag = sb("rs_diag", [P, 2, CH])
        xn = sb("xn", [P, 2, CH])
        mhalf = sb("mhalf", [P, 1])
        qk = sb("qk", [P, 2, 2, CH])
        qkn = sb("qkn", [P, 2, 2, CH])
        rest = sb("rest", [P, 2, 2, CH])
        hml = sb("hml", [P, 2, PARTS, 2, CH], BF16)
        vn = sb("vn", [P, 2, CH // P, KF])
        if rms:
            sqqk = sb("sqqk", [P, 2, 2, CH])
            NMS = 2 * CH // P * HEADS
            ms = sb("ms", [P, 2, NMS])
            rms_sb = sb("rms_sb", [P, 2, NMS])
            rinv = sb("rinv", [P, 2, NMS])
            rinv_wide = sb("rinv_wide", [P, 2, 2, CH // P, P])
            w_sb = sb("w_sb", [P, 3 * P])
            bias = sb("bias", [P, 2])
            vbias = sb("vbias", [P, P])
            head_mean = sb("head_mean", [P, HEADS])
            gain = sb("gain", [P, 2])
        else:
            w_down = sb("w_down", [P, LAT])
            w_q = sb("w_q", [LAT, P])
            w_kv = sb("w_kv", [LAT, 2 * HD])
            lat = sb("lat", [LAT, 2, CH])
        pA = [ps(f"pA{u}", [P, CH]) for u in range(2)]
        pQ = [ps(f"pQ{u}", [P, CH]) for u in range(2)]
        pK = [ps(f"pK{u}", [P, CH]) for u in range(2)]
        pV = [ps(f"pV{u}", [P, CH]) for u in range(2)]
        w_loaded, mhalf_set = sem("w_loaded"), sem("mhalf_set")
        mean_ready, cen_ready, sq_ready, var_ready = (sem2(n) for n in ("mean_r", "cen_r", "sq_r", "var_r"))
        ve_ready, rs_ready, xn_ready, qkv_ready = (sem2(n) for n in ("ve_r", "rs_r", "xn_r", "qkv_r"))
        lat_ps, lat_ready, vn_ready, squares_ready = (sem2(n) for n in ("lat_p", "lat_r", "vn_r", "squares_r"))
        diag_ready, rs_spread = sem2("diag_r"), sem2("rs_spread")
        ms_ready, ms_read, rms_ready, rinv_ready = (sem2(n) for n in ("ms_r", "ms_read", "rms_r", "rinv_r"))
        wide_ready, rms_spread, qkn_ready = (sem2(n) for n in ("wide_r", "rms_spread", "qkn_r"))
        hi_ready, rest_ready, mid_ready, lo_ready = (sem2(n) for n in ("hi_r", "rest_r", "mid_r", "lo_r"))
        parts_stored, v_stored = sem2("parts_st"), sem2("v_st")
        n_w = 7 if rms else 3
        sides = ((0, P), (1, KF))

        def sq_cols(u):
            return sqqk[:, u].rearrange("p s n -> p (s n)")

        block = ctx.enter_context(nc.Block())

        @block.sync
        def _(sp):
            if rms:
                sp.dma_start(w_sb[:, :], w["Wqkv_t"]).then_inc(w_loaded, 16)
                sp.dma_start(bias[:, 0:1], w["bqkv"][0:P, :]).then_inc(w_loaded, 16)
                sp.dma_start(bias[:, 1:2], w["bqkv"][P:2 * P, :]).then_inc(w_loaded, 16)
                sp.dma_start(vbias[:, :], w["bv_row"].to_broadcast([P, P])).then_inc(w_loaded, 16)
                sp.dma_start(head_mean[:, :], w["head_mean"]).then_inc(w_loaded, 16)
                sp.dma_start(gain[:, 0:1], w["wq"]).then_inc(w_loaded, 16)
                sp.dma_start(gain[:, 1:2], w["wk"]).then_inc(w_loaded, 16)
            else:
                sp.dma_start(w_down[:, :], w["w_down"]).then_inc(w_loaded, 16)
                sp.dma_start(w_q[:, :], w["w_q"]).then_inc(w_loaded, 16)
                sp.dma_start(w_kv[:, :], w["w_kv"]).then_inc(w_loaded, 16)
            with sp.Fori(0, NCH // 2) as cc:
                for u in range(2):
                    cols = ds((2 * cc + u) * CH, CH)
                    sp.wait_ge(vn_ready[u], cc + 1)
                    sp.dma_start(v_rows[cols, :].rearrange("(t p) f -> p t f", p=P), vn[:, u]).then_inc(v_stored[u], 16)
                for u in range(2):
                    cols = ds((2 * cc + u) * CH, CH)
                    stores = [(dst[:, :, cols].rearrange("a f n -> f a n"), hml[0:rows, u, :, s, :])
                              for (s, rows), dst in zip(sides, (q_parts, k_parts))]
                    sp.compute_val((2 * cc + u) * CH * 2)
                    sp.wait_ge(lo_ready[u], cc + 1)
                    for dst, src in stores:
                        sp.dma_start(dst, src).then_inc(parts_stored[u], 16)
            for u in range(2):
                sp.wait_ge(v_stored[u], 16 * (NCH // 2))
                sp.wait_ge(parts_stored[u], 16 * 2 * (NCH // 2))

        def pipeline(eng, norm, main):
            for _ in norm(0):
                pass
            with eng.Fori(0, PAIRS - 1) as cc:
                main(cc, norm(cc + 1))
            main(PAIRS - 1, iter(()))

        @block.tensor
        def _(pe):
            def norm(cc):
                for u in range(2):
                    pe.wait_ge(xn_ready[u], cc)
                    pe.matmul(pA[u][:, :], ones_mean[:, :], XR[:, ds((2 * cc + u) * CH, CH)],
                              start=True, stop=True).then_inc(mean_ready[u], 1)
                yield
                for u in range(2):
                    pe.wait_ge(sq_ready[u], cc + 1)
                    for t in range(CH // P):
                        mm = pe.matmul(pA[u][:, t:t + 1], sq[:, u, t * P:(t + 1) * P], ones_mean[:, 0:1], start=True, stop=True)
                    mm.then_inc(var_ready[u], 1)
                yield
                for u in range(2):
                    pe.wait_ge(diag_ready[u], cc + 1)
                    pe.matmul(pA[u][:, :], ones[:, :], rs_diag[:, u], start=True, stop=True).then_inc(rs_spread[u], 1)
                yield

            def main(cc, ahead):
                for u in range(2):
                    pe.wait_ge(xn_ready[u], cc + 1)
                    pe.wait_ge(qkn_ready[u], cc)
                    pe.wait_ge(vn_ready[u], cc)
                    if rms:
                        pe.matmul(pQ[u][:, :], w_sb[:, 0:P], xn[:, u], start=True, stop=True)
                        pe.matmul(pK[u][:, :], w_sb[:, P:2 * P], xn[:, u], start=True, stop=True)
                        for t in range(CH // P):
                            mm = pe.matmul(pV[u][:, t * P:(t + 1) * P], xn[:, u, t * P:(t + 1) * P],
                                           w_sb[:, 2 * P:3 * P], start=True, stop=True)
                        mm.then_inc(qkv_ready[u], 1)
                    else:
                        pe.matmul(pK[u][0:LAT, :], w_down[:, :], xn[:, u], start=True, stop=True).then_inc(lat_ps[u], 1)
                next(ahead, None)
                for u in range(2):
                    if rms:
                        pe.wait_ge(squares_ready[u], cc + 1)
                        for k in range(2 * CH // P):
                            mm = pe.matmul(pQ[u][:, k * HEADS:(k + 1) * HEADS], sq_cols(u)[:, k * P:(k + 1) * P],
                                           head_mean[:, :], start=True, stop=True)
                        mm.then_inc(ms_ready[u], 1)
                    else:
                        pe.wait_ge(lat_ready[u], cc + 1)
                        pe.matmul(pQ[u][:, :], w_q[:, :], lat[:, u], start=True, stop=True)
                        pe.matmul(pK[u][0:HD, :], w_kv[:, 0:HD], lat[:, u], start=True, stop=True)
                        for t in range(CH // P):
                            mm = pe.matmul(pV[u][:, t * HD:(t + 1) * HD], lat[:, u, t * P:(t + 1) * P],
                                           w_kv[:, HD:2 * HD], start=True, stop=True)
                        mm.then_inc(qkv_ready[u], 1)
                next(ahead, None)
                if rms:
                    for u in range(2):
                        pe.wait_ge(wide_ready[u], cc + 1)
                        for s, dst in ((0, pQ[u]), (1, pK[u])):
                            for t in range(CH // P):
                                mm = pe.matmul(dst[:, t * P:(t + 1) * P], rinv_wide[:, u, s, t], ident[:, :],
                                               start=True, stop=True)
                        mm.then_inc(rms_spread[u], 1)
                next(ahead, None)

            pe.wait_ge(w_loaded, 16 * n_w)
            pipeline(pe, norm, main)

        @block.vector
        def _(dve):
            def norm(cc):
                for u in range(2):
                    dve.wait_ge(mean_ready[u], cc + 1)
                    dve.tensor_tensor(cen[:, u], XR[:, ds((2 * cc + u) * CH, CH)], pA[u][:, :],
                                      ALU.subtract).then_inc(cen_ready[u], 1)
                yield
                for u in range(2):
                    dve.wait_ge(var_ready[u], cc + 1)
                    dve.tensor_scalar(ve[:, u], pA[u][:, 0:CH // P], LN_EPS, None, ALU.add).then_inc(ve_ready[u], 1)
                yield
                for u in range(2):
                    dve.wait_ge(rs_ready[u], cc + 1)
                    for t in range(CH // P):
                        mm = dve.tensor_scalar(rs_diag[:, u, t * P:(t + 1) * P], ident[:, :], rs[:, u, t:t + 1], None, ALU.mult)
                    mm.then_inc(diag_ready[u], 1)
                yield
                for u in range(2):
                    dve.wait_ge(rs_spread[u], cc + 1)
                    dve.tensor_tensor(xn[:, u], cen[:, u], pA[u][:, :], ALU.mult).then_inc(xn_ready[u], 1)
                yield

            def main(cc, ahead):
                next(ahead, None)
                for u in range(2):
                    dve.wait_ge(v_stored[u], 16 * cc)
                    dve.wait_ge(qkv_ready[u], cc + 1)
                    v_ps = pV[u][:, 0:CH // P * KF].rearrange("p (t f) -> p t f", f=KF)
                    if rms:
                        dve.tensor_tensor(vn[:, u], v_ps, bcast_mid(vbias[:, :], CH // P), ALU.add).then_inc(vn_ready[u], 1)
                    else:
                        dve.tensor_copy(vn[:, u], v_ps).then_inc(vn_ready[u], 1)
                if rms:
                    for u in range(2):
                        dve.wait_ge(ms_ready[u], cc + 1)
                        dve.tensor_scalar(ms[:, u], pQ[u][:, 0:NMS], RMS_EPS, None, ALU.add).then_inc(ms_read[u], 1)
                    next(ahead, None)
                    for u in range(2):
                        dve.wait_ge(rms_ready[u], cc + 1)
                        dve.reciprocal(rinv[:, u], rms_sb[:, u]).then_inc(rinv_ready[u], 1)
                        dve.wait_ge(rinv_ready[u], cc + 1)
                        dve.tensor_copy(rinv_wide[:, u].rearrange("p s t (h d) -> p (s t h) d", d=HD),
                                        bcast_last(rinv[:, u], HD)).then_inc(wide_ready[u], 1)
                    next(ahead, None)
                    for u in range(2):
                        dve.wait_ge(rms_spread[u], cc + 1)
                        for s, src in ((0, pQ[u]), (1, pK[u])):
                            mm = dve.scalar_tensor_tensor(out=qkn[:, u, s], in0=qk[:, u, s], scalar=gain[:, s:s + 1],
                                                          in1=src[:, :], op0=ALU.mult, op1=ALU.mult)
                        mm.then_inc(qkn_ready[u], 1)
                    next(ahead, None)
                for u in range(2):
                    dve.wait_ge(hi_ready[u], cc + 1)
                    for s, rows in sides:
                        mm = dve.tensor_tensor(rest[0:rows, u, s], qkn[0:rows, u, s], hml[0:rows, u, 0, s], ALU.subtract)
                    mm.then_inc(rest_ready[u], 1)
                next(ahead, None)
                for u in range(2):
                    dve.wait_ge(mid_ready[u], cc + 1)
                    for s, rows in sides:
                        mm = dve.tensor_tensor(hml[0:rows, u, 2, s], rest[0:rows, u, s], hml[0:rows, u, 1, s], ALU.subtract)
                    mm.then_inc(lo_ready[u], 1)
                for _ in ahead:
                    pass

            dve.wait_ge(w_loaded, 16 * n_w)
            pipeline(dve, norm, main)

        @block.scalar
        def _(act):
            def norm(cc):
                for u in range(2):
                    act.wait_ge(cen_ready[u], cc + 1)
                    act.activation(sq[:, u], cen[:, u], ACT.Square).then_inc(sq_ready[u], 1)
                yield

            def main(cc, ahead):
                if not rms:
                    for u in range(2):
                        act.wait_ge(lat_ps[u], cc + 1)
                        act.activation(lat[:, u], pK[u][0:LAT, :], ACT.Copy).then_inc(lat_ready[u], 1)
                for u in range(2):
                    act.wait_ge(qkv_ready[u], cc + 1)
                    if rms:
                        for s, src in ((0, pQ[u]), (1, pK[u])):
                            act.activation(qk[:, u, s], src[:, :], ACT.Identity, bias=bias[:, s:s + 1])
                            mm = act.activation(sqqk[:, u, s], src[:, :], ACT.Square, bias=bias[:, s:s + 1])
                        mm.then_inc(squares_ready[u], 1)
                    else:
                        act.activation(qkn[:, u, 0], pQ[u][:, :], ACT.Copy, scale=float(HD) ** -0.5)
                        act.activation(qkn[0:HD, u, 1], pK[u][0:HD, :], ACT.Copy).then_inc(qkn_ready[u], 1)
                next(ahead, None)
                if rms:
                    for u in range(2):
                        act.wait_ge(ms_read[u], cc + 1)
                        act.activation(rms_sb[:, u], ms[:, u], ACT.Sqrt).then_inc(rms_ready[u], 1)
                for u in range(2):
                    act.wait_ge(parts_stored[u], 16 * 2 * cc)
                    act.wait_ge(qkn_ready[u], cc + 1)
                    for s, rows in sides:
                        mm = act.activation(hml[0:rows, u, 0, s], qkn[0:rows, u, s], ACT.Copy)
                    mm.then_inc(hi_ready[u], 1)
                for u in range(2):
                    act.wait_ge(rest_ready[u], cc + 1)
                    for s, rows in sides:
                        mm = act.activation(hml[0:rows, u, 1, s], rest[0:rows, u, s], ACT.Copy)
                    mm.then_inc(mid_ready[u], 1)

            act.wait_ge(w_loaded, 16 * n_w)
            pipeline(act, norm, main)

        @block.gpsimd
        def _(pool):
            pool.memset(mhalf[:, :], -0.5).then_inc(mhalf_set, 1)
            pool.wait_ge(mhalf_set, 1)
            with pool.Fori(0, NCH // 2) as cc:
                for u in range(2):
                    pool.wait_ge(ve_ready[u], cc + 1)
                    pool.tensor_tensor(rs[:, u], ve[:, u], mhalf[:, :].to_broadcast([P, CH // P]), ALU.pow).then_inc(rs_ready[u], 1)


def attend(nc, tag, XR, ident, w, q_parts, k_parts, v_rows, causal, many_keys):
    KH = GRP if many_keys else 1
    NQH = SEQ // CH
    units = [(qh, kt) for qh in range(NQH) for kt in range(QT) if not causal or kt * P < (qh + 1) * CH]
    first_col = {(qh, kt): max(0, kt * P - qh * CH) if causal else 0 for qh, kt in units}
    max_units = []
    for j in range(GRP):
        for qt in range(QT):
            for kh in range(NQH):
                width = min(CH, (qt + 1) * P - kh * CH) if causal else CH
                if width > 0:
                    max_units.append((j, qt, kh, width))
    NU, NM = len(units), len(max_units)
    STEPS = BATCH * NGRP
    with ExitStack() as ctx:
        sb, ps, sem, sem2 = alloc(ctx, nc, tag)
        QS = sb("QS", [KROWS, NGRP, GRP, SEQ], BF16)
        KS = sb("KS", [KROWS, NGRP, KH, SEQ], BF16)
        VS = sb("VS", [P, NGRP, QT, KH, 32])
        ones_row = sb("ones_row", [PARTS, KH, SEQ], BF16)
        zero_row = sb("zero_row", [PARTS, GRP, SEQ], BF16)
        PT = sb("PT", [P, 4, 2, CH])
        row_max = sb("row_max", [P, GRP * QT, NQH])
        neg_max = sb("neg_max", [P, GRP * QT])
        shift = sb("shift", [GRP * QT, P])
        shift_rest = sb("shift_rest", [GRP * QT, P])
        shift_parts = sb("shift_parts", [GRP * QT, PARTS, P], BF16)
        z_sb = sb("z_sb", [P, 2, NQH, CH])
        NDEN = GRP * SEQ // P
        den = sb("den", [P, NDEN])
        den_inv = sb("den_inv", [P, NDEN])
        inv_rows = sb("inv_rows", [P, NQH, CH])
        ZN = sb("ZN", [P, NGRP, SEQ])
        spread_den = sb("spread_den", [P, P])
        wo = sb("wo", [P, NGRP, P])
        bo = sb("bo", [P, 1])
        if causal:
            mask_f = sb("mask_f", [P, 2, P])
            mask = sb("mask", [P, 2, P], BF16)
            ident_b = sb("ident_b", [P, P], BF16)
        pS = [ps(f"pS{v}", [P, 2, CH]) for v in range(2)]
        pM = [ps(f"pM{v}", [P, CH]) for v in range(2)]
        pZ = ps("pZ", [P, CH])
        pX = ps("pX", [P, CH])
        w_loaded, consts_set, masks_set, stacks_zeroed = sem("w_loaded"), sem("consts_set"), sem("masks_set"), sem("stacks_zeroed")
        q_loaded, k_loaded, v_loaded, shift_placed = ([sem(f"{s}{g}") for g in range(NGRP)] for s in ("q_l", "k_l", "v_l", "shift_p"))
        max_scores, max_read, neg_ready = sem("max_scores"), sem("max_read"), sem("neg_ready")
        shift_t, shift_copied, shift_hi, shift_r, shift_mid, shift_done = (
            sem(n) for n in ("shift_t", "shift_c", "shift_hi", "shift_r", "shift_mid", "shift_done"))
        scores, exps, pv_done = sem("scores"), sem("exps"), sem("pv_done")
        z_copied, den_placed, inv_ready, inv_placed, inv_spread, zn_ready = (
            sem(n) for n in ("z_copied", "den_placed", "inv_ready", "inv_placed", "inv_spread", "zn_ready"))
        wo_ps, wo_added, rows_set = sem("wo_ps"), sem("wo_added"), sem("rows_set")
        block = ctx.enter_context(nc.Block())
        LAST = BATCH - 1

        def batches(eng, body):
            body(0, True, False)
            with eng.Fori(1, LAST) as b:
                body(b, False, False)
            body(LAST, False, True)

        @block.sync
        def _(sp):
            sp.dma_start(wo[:, :, :], w["wo_pad"]).then_inc(w_loaded, 16)
            sp.dma_start(spread_den[:, :], w["spread_den"]).then_inc(w_loaded, 16)
            if causal:
                sp.dma_start(mask_f[:, :, :], w["causal"]).then_inc(w_loaded, 16)
            else:
                sp.dma_start(bo[:, :], w["bo"]).then_inc(w_loaded, 16)

            def load(b, g, first=False):
                v = g
                cols = ds(b * SEQ, SEQ)
                sp.dma_start(QS[STACK:STACK + PARTS, v], zero_row[:, :, :]).then_inc(q_loaded[v], 16)
                for a in range(PARTS):
                    rows = slice(a * PARTS * HD, (a + 1) * PARTS * HD)
                    for c in range(PARTS):
                        r = (a * PARTS + c) * HD
                        sp.dma_start(QS[r:r + HD, v],
                                     q_parts[a, g * GRP * HD:(g + 1) * GRP * HD, cols].rearrange("(j d) n -> d j n", d=HD)
                                     ).then_inc(q_loaded[v], 16)
                        if many_keys:
                            sp.dma_start(KS[r:r + HD, v],
                                         k_parts[c, g * GRP * HD:(g + 1) * GRP * HD, cols].rearrange("(j d) n -> d j n", d=HD)
                                         ).then_inc(k_loaded[v], 16)
                    if not many_keys:
                        sp.dma_start(KS[rows, v, 0], k_parts[:, :, cols]).then_inc(k_loaded[v], 16)
                if first:
                    sp.wait_ge(consts_set, 3)
                vs = v_rows[cols, g * GRP * HD:(g + 1) * GRP * HD] if many_keys else v_rows[cols, :]
                for j in range(KH):
                    sp.dma_start(VS[:, v, :, j, 0:HD], vs[:, j * HD:(j + 1) * HD].rearrange("(t p) d -> p t d", p=P)
                                 ).then_inc(v_loaded[v], 16)

            def place_shift(g, n):
                v = g
                sp.wait_ge(shift_done, n + 1)
                for a in range(PARTS):
                    sp.dma_start(QS[STACK + a:STACK + a + 1, v].rearrange("o j (t q) -> o (j t) q", q=P),
                                 shift_parts[:, a, :]).then_inc(shift_placed[v], 16)

            def load_first(g):
                sp.wait_ge(stacks_zeroed, 2 * (g + 1) + 2)
                sp.dma_start(KS[STACK:STACK + PARTS, g], ones_row[:, :, :]).then_inc(k_loaded[g], 16)
                load(0, g, True)

            load_first(0)
            load_first(1)
            place_shift(0, 0)
            load_first(2)
            load_first(3)

            def invert(g, n):
                sp.wait_ge(z_copied, NQH * (n + 1))
                for j in range(GRP):
                    r = 32 * j + HD
                    sp.dma_start(den[32 * j:32 * j + 32, :], z_sb[r:r + 1, g % 2].rearrange("o h (p n) -> o (h p) n", n=NDEN)
                                 ).then_inc(den_placed, 16)
                sp.wait_ge(inv_ready, n + 1)
                for j in range(GRP):
                    r = 32 * j + HD
                    sp.dma_start(inv_rows[r:r + 1].rearrange("o h (p n) -> o (h p) n", n=NDEN), den_inv[32 * j:32 * j + 32, :]
                                 ).then_inc(inv_placed, 16)

            def body(b, first, last):
                for g in range(NGRP):
                    n = b * NGRP + g
                    if g > 0 or not first:
                        invert((g - 1) % NGRP, n - 1)
                        if g == 0 or not last:
                            sp.wait_ge(pv_done, n * NU)
                            load(b + 1 if g > 0 else b, (g - 1) % NGRP)
                    if not (last and g == NGRP - 1):
                        place_shift((g + 1) % NGRP, n + 1)
                if last:
                    invert(NGRP - 1, b * NGRP + NGRP - 1)
            batches(sp, body)

        def spread(pe, b, n, qh):
            pe.wait_ge(inv_placed, 16 * GRP * (n + 1))
            pe.wait_ge(zn_ready, n * NQH + qh)
            pe.wait_ge(wo_added, NQH * b)
            pe.matmul(pX[:, :], spread_den[:, :], inv_rows[:, qh], start=True, stop=True).then_inc(inv_spread, 1)

        SLOTS = 5
        EARLY_SLOTS = 13 if causal else 8
        AT_INVERT, AT_HALF = NM // 5, [NM // 2, 5 * NM // 8]
        AT_WO = [3 * NM // 4, 7 * NM // 8]

        def project(pe, b, c):
            pe.wait_ge(zn_ready, NQH * NGRP * (b + 1))
            pe.wait_ge(wo_added, NQH * b + c)
            for g in range(NGRP):
                mm = pe.matmul(pX[:, :], wo[:, g], ZN[:, g, c * CH:(c + 1) * CH], start=(g == 0), stop=(g == NGRP - 1))
            mm.then_inc(wo_ps, 1)

        def max_pass(pe, b, g, n, before=None):
            v = g
            pe.wait_ge(shift_copied, n)
            pe.wait_ge(q_loaded[v], 16 * (1 + PARTS * PARTS) * (b + 1))
            pe.wait_ge(k_loaded[v], 16 + 16 * (PARTS * PARTS if many_keys else PARTS) * (b + 1))
            for i, (j, qt, kh, width) in enumerate(max_units):
                m = i % 2
                if before and i in AT_HALF:
                    spread(pe, before[0], before[2], AT_HALF.index(i))
                if before and before[1] == NGRP - 1 and i in AT_WO:
                    project(pe, before[0], AT_WO.index(i))
                pe.wait_ge(max_read, n * NM + max(i - 1, 0))
                diag = causal and (qt + 1) * P - kh * CH <= CH
                mm = pe.matmul(pM[m][:, 0:width], QS[:, v, j, qt * P:(qt + 1) * P],
                               KS[:, v, j if many_keys else 0, kh * CH:kh * CH + width], start=True, stop=not diag)
                if diag:
                    mm = pe.matmul(pM[m][:, width - P:width], ident_b[:, :], mask[:, 1], start=False, stop=True)
                mm.then_inc(max_scores, 1)
                yield 1
            pe.wait_ge(neg_ready, n + 1)
            pe.transpose(pM[0][0:GRP * QT, 0:P], neg_max[:, :], ident[:, :]).then_inc(shift_t, 1)
            yield 1

        @block.tensor
        def _(pe):
            pe.wait_ge(w_loaded, 48)
            if causal:
                pe.wait_ge(masks_set, 2)
            for _ in max_pass(pe, 0, 0, 0):
                pass

            def step(b, g, n, ahead, before):
                v = g
                pe.wait_ge(shift_placed[v], 48 * (b + 1))
                pe.wait_ge(v_loaded[v], 16 * KH * (b + 1))
                maxima = max_pass(pe, *ahead, before) if ahead else iter(())
                taken = 0

                def some_maxima(slots):
                    nonlocal taken
                    due = -(-slots * (NM + 1) // (SLOTS * NU - EARLY_SLOTS))
                    while taken < due:
                        next(maxima, None)
                        taken += 1

                def pv(i):
                    qh, kt = units[i]
                    c0 = first_col[qh, kt]
                    if kt == 0:
                        pe.wait_ge(z_copied, n * NQH + qh)
                    last_kt = i + 1 == NU or units[i + 1][0] != qh
                    pe.wait_ge(exps, 2 * (n * NU + i) + 2)
                    for j in range(GRP):
                        slot = (2 * i + j // 2) % 4
                        mm = pe.matmul(pZ[32 * j:32 * j + 32, c0:CH], VS[:, v, kt, j if many_keys else 0, :],
                                       PT[:, slot, j % 2, c0:CH], start=(kt == 0), stop=last_kt)
                    mm.then_inc(pv_done, 1)

                for i, (qh, kt) in enumerate(units):
                    c0 = first_col[qh, kt]
                    q0 = qh * CH + c0
                    diag = causal and kt * P >= qh * CH
                    for h in range(2):
                        pe.wait_ge(exps, 2 * n * NU + max(2 * i + h - 1, 0))
                        for k in range(2):
                            j = 2 * h + k
                            mm = pe.matmul(pS[h][:, k, c0:CH], KS[:, v, j if many_keys else 0, kt * P:(kt + 1) * P],
                                           QS[:, v, j, q0:(qh + 1) * CH], start=True, stop=not diag)
                            if diag:
                                mm = pe.matmul(pS[h][:, k, c0:c0 + P], ident_b[:, :], mask[:, 0], start=False, stop=True)
                            if k == 1:
                                mm.then_inc(scores, 1)
                            some_maxima(SLOTS * i + 2 * h + k + 1)
                    if not ahead and i == NU // 2:
                        for half in range(NQH):
                            spread(pe, before[0], before[2], half)
                    if i > 0:
                        pv(i - 1)
                    some_maxima(SLOTS * (i + 1))
                for _ in maxima:
                    pass
                pv(NU - 1)

            def body(b, first, last):
                for g in range(NGRP):
                    n = b * NGRP + g
                    ahead = None if last and g == NGRP - 1 else (b + (g + 1) // NGRP, (g + 1) % NGRP, n + 1)
                    before = None if first and g == 0 else (b if g > 0 else b - 1, (g - 1) % NGRP, n - 1)
                    step(b, g, n, ahead, before)
                if last:
                    for qh in range(NQH):
                        spread(pe, b, n, qh)
                    for c in range(NQH):
                        project(pe, b, c)
            batches(pe, body)

        @block.scalar
        def _(act):
            def body(b, first, last):
                for g in range(NGRP):
                    n = b * NGRP + g

                    def copy_z(qh):
                        act.wait_ge(pv_done, n * NU + max(i for i, u in enumerate(units) if u[0] == qh) + 1)
                        act.activation(z_sb[:, g % 2, qh], pZ[:, :], ACT.Copy).then_inc(z_copied, 1)

                    if not (first and g == 0):
                        act.wait_ge(zn_ready, (n - 1) * NQH)
                    for i, (qh, kt) in enumerate(units):
                        c0 = first_col[qh, kt]
                        for h in range(2):
                            act.wait_ge(pv_done, n * NU + max(i - 1, 0))
                            act.wait_ge(scores, 2 * (n * NU + i) + h + 1)
                            act.activation(PT[:, (2 * i + h) % 4, :, c0:CH], pS[h][:, :, c0:CH], ACT.Exp).then_inc(exps, 1)
                        if qh > 0 and kt == 0:
                            copy_z(qh - 1)
                    copy_z(NQH - 1)
            act.wait_ge(w_loaded, 48)
            batches(act, body)

        @block.gpsimd
        def _(pool):
            pool.memset(VS[:, :, :, :, :], 0.0).then_inc(consts_set, 1)
            pool.wait_ge(consts_set, 1)
            pool.memset(VS[:, :, :, :, HD:HD + 1].rearrange("p v t j o -> p (v t j) o"), 1.0).then_inc(consts_set, 1)
            pool.memset(inv_rows[:, :, :], 0.0).then_inc(consts_set, 1)

        @block.vector
        def _(dve):
            dve.memset(zero_row[:, :, :], 0.0).then_inc(stacks_zeroed, 1)
            dve.memset(ones_row[:, :, :], 1.0).then_inc(stacks_zeroed, 1)
            for v in range(NGRP):
                dve.memset(QS[:, v], 0.0).then_inc(stacks_zeroed, 1)
                dve.memset(KS[:, v], 0.0).then_inc(stacks_zeroed, 1)
            dve.wait_ge(w_loaded, 48)
            if causal:
                dve.tensor_copy(mask[:, :, :], mask_f[:, :, :]).then_inc(masks_set, 1)
                dve.tensor_copy(ident_b[:, :], ident[:, :]).then_inc(masks_set, 1)

            def invert(n):
                dve.wait_ge(den_placed, 16 * GRP * (n + 1))
                dve.reciprocal(den_inv[:, :], den[:, :]).then_inc(inv_ready, 1)

            def normalise(b, g, n, halves=range(NQH)):
                for qh in halves:
                    dve.wait_ge(wo_ps, NQH * b)
                    dve.wait_ge(inv_spread, n * NQH + qh + 1)
                    dve.tensor_tensor(ZN[:, g, qh * CH:(qh + 1) * CH], z_sb[:, g % 2, qh], pX[:, :], ALU.mult).then_inc(zn_ready, 1)

            def add_projection(b, c):
                cols = ds(b * SEQ + c * CH, CH)
                dve.wait_ge(wo_ps, NQH * b + c + 1)
                if causal:
                    dve.tensor_tensor(XR[:, cols], XR[:, cols], pX[:, :], ALU.add).then_inc(wo_added, 1)
                else:
                    dve.scalar_tensor_tensor(out=XR[:, cols], in0=pX[:, :], scalar=bo[:, :], in1=XR[:, cols],
                                             op0=ALU.add, op1=ALU.add).then_inc(wo_added, 1)

            def maxima(g, n, before, middle=None):
                for i, (j, qt, kh, width) in enumerate(max_units):
                    if middle and i == AT_INVERT:
                        invert(middle[2])
                    if middle and i in AT_HALF:
                        normalise(*middle, [AT_HALF.index(i)])
                    if middle and middle[1] == NGRP - 1 and i in AT_WO:
                        add_projection(middle[0], AT_WO.index(i))
                    dve.wait_ge(max_scores, n * NM + i + 1)
                    dve.tensor_reduce(row_max[:, j * QT + qt, kh:kh + 1], pM[i % 2][:, 0:width], AX.X, ALU.max).then_inc(max_read, 1)
                dve.wait_ge(max_read, (n + 1) * NM)
                dve.wait_ge(shift_t, n)
                dve.tensor_reduce(neg_max[:, :], row_max[:, :, :], AX.X, ALU.max, negate=True).then_inc(neg_ready, 1)
                dve.wait_ge(shift_t, n + 1)
                dve.tensor_copy(shift[:, :], pM[0][0:GRP * QT, 0:P]).then_inc(shift_copied, 1)
                dve.wait_ge(shift_copied, n + 1)
                if before:
                    dve.wait_ge(shift_placed[before[0]], 48 * before[1])
                dve.tensor_copy(shift_parts[:, 0], shift[:, :]).then_inc(shift_hi, 1)
                dve.wait_ge(shift_hi, n + 1)
                dve.tensor_tensor(shift_rest[:, :], shift[:, :], shift_parts[:, 0], ALU.subtract).then_inc(shift_r, 1)
                dve.wait_ge(shift_r, n + 1)
                dve.tensor_copy(shift_parts[:, 1], shift_rest[:, :]).then_inc(shift_mid, 1)
                dve.wait_ge(shift_mid, n + 1)
                dve.tensor_tensor(shift_parts[:, 2], shift_rest[:, :], shift_parts[:, 1], ALU.subtract).then_inc(shift_done, 1)

            if causal:
                dve.memset(row_max[:, :, :], 2 * NEG).then_inc(rows_set, 1)
                dve.wait_ge(rows_set, 1)
            maxima(0, 0, None)

            def body(b, first, last):
                for g in range(NGRP):
                    n = b * NGRP + g
                    before = None if first and g == 0 else (b if g > 0 else b - 1, (g - 1) % NGRP, n - 1)
                    if not (last and g == NGRP - 1):
                        maxima((g + 1) % NGRP, n + 1, (g, b + 1), before)
                    else:
                        invert(n - 1)
                        normalise(*before)
                if last:
                    invert(n)
                    normalise(b, NGRP - 1, n)
                    for c in range(NQH):
                        add_projection(b, c)
            batches(dve, body)


def layer_norm_all(nc, tag, src, dst, ident, ones, ones_mean):
    LANES = 4
    with ExitStack() as ctx:
        sb, ps, sem, sem2 = alloc(ctx, nc, tag)
        cen = sb("cen", [P, LANES, CH])
        sq = sb("sq", [P, LANES, CH])
        ve = sb("ve", [P, LANES, CH // P])
        rs = sb("rs", [P, LANES, CH // P])
        rs_diag = sb("rs_diag", [P, LANES, CH])
        mhalf = sb("mhalf", [P, 1])
        pA = [ps(f"pA{u}", [P, CH]) for u in range(LANES)]
        mhalf_set = sem("mhalf_set")

        def sems(name):
            return [sem(f"{name}{u}") for u in range(LANES)]

        mean_ready, cen_ready, sq_ready, var_ready = (sems(n) for n in ("mean_r", "cen_r", "sq_r", "var_r"))
        ve_ready, rs_ready, diag_ready, rs_spread, done = (sems(n) for n in ("ve_r", "rs_r", "diag_r", "rs_spread", "done"))
        block = ctx.enter_context(nc.Block())

        @block.tensor
        def _(pe):
            with pe.Fori(0, NCH // LANES) as cc:
                for u in range(LANES):
                    pe.wait_ge(done[u], cc)
                    pe.matmul(pA[u][:, :], ones_mean[:, :], src[:, ds((LANES * cc + u) * CH, CH)],
                              start=True, stop=True).then_inc(mean_ready[u], 1)
                for u in range(LANES):
                    pe.wait_ge(sq_ready[u], cc + 1)
                    for t in range(CH // P):
                        mm = pe.matmul(pA[u][:, t:t + 1], sq[:, u, t * P:(t + 1) * P], ones_mean[:, 0:1], start=True, stop=True)
                    mm.then_inc(var_ready[u], 1)
                for u in range(LANES):
                    pe.wait_ge(diag_ready[u], cc + 1)
                    pe.matmul(pA[u][:, :], ones[:, :], rs_diag[:, u], start=True, stop=True).then_inc(rs_spread[u], 1)

        @block.vector
        def _(dve):
            with dve.Fori(0, NCH // LANES) as cc:
                for u in range(LANES):
                    dve.wait_ge(mean_ready[u], cc + 1)
                    dve.tensor_tensor(cen[:, u], src[:, ds((LANES * cc + u) * CH, CH)], pA[u][:, :],
                                      ALU.subtract).then_inc(cen_ready[u], 1)
                for u in range(LANES):
                    dve.wait_ge(var_ready[u], cc + 1)
                    dve.tensor_scalar(ve[:, u], pA[u][:, 0:CH // P], LN_EPS, None, ALU.add).then_inc(ve_ready[u], 1)
                for u in range(LANES):
                    dve.wait_ge(rs_ready[u], cc + 1)
                    for t in range(CH // P):
                        mm = dve.tensor_scalar(rs_diag[:, u, t * P:(t + 1) * P], ident[:, :], rs[:, u, t:t + 1], None, ALU.mult)
                    mm.then_inc(diag_ready[u], 1)
                for u in range(LANES):
                    dve.wait_ge(rs_spread[u], cc + 1)
                    dve.tensor_tensor(dst[:, ds((LANES * cc + u) * CH, CH)], cen[:, u], pA[u][:, :], ALU.mult).then_inc(done[u], 1)

        @block.scalar
        def _(act):
            with act.Fori(0, NCH // LANES) as cc:
                for u in range(LANES):
                    act.wait_ge(cen_ready[u], cc + 1)
                    act.activation(sq[:, u], cen[:, u], ACT.Square).then_inc(sq_ready[u], 1)

        @block.gpsimd
        def _(pool):
            pool.memset(mhalf[:, :], -0.5).then_inc(mhalf_set, 1)
            pool.wait_ge(mhalf_set, 1)
            with pool.Fori(0, NCH // LANES) as cc:
                for u in range(LANES):
                    pool.wait_ge(ve_ready[u], cc + 1)
                    pool.tensor_tensor(rs[:, u], ve[:, u], mhalf[:, :].to_broadcast([P, CH // P]), ALU.pow).then_inc(rs_ready[u], 1)


DEPTH = 6
LH, LD = 16, 64
INNER = LH * LD
WIN = 32
NW = P // WIN
HP = LH // 2
NT = TOK // P
FF = 341
FT = 3
FROWS = [P, P, FF - 2 * P]
NS = 9
L2_MIN = 1e-24


def local_transformer(nc, d, XR, ident, ones, ones_mean):
    with ExitStack() as outer:
        X = outer.enter_context(nc.sbuf_tensor("lt_X", [P, TOK], F32))
        layer_norm_all(nc, "lt_ln", XR, X, ident, ones, ones_mean)
        v_dram = nc.dram_tensor("lt_v", (WIN + TOK, INNER), F32, kind="Internal").ap()
        local_layers(nc, d, XR, X, ident, ones, ones_mean, v_dram)


def local_layers(nc, d, XR, X, ident, ones, ones_mean, v_dram):
    with ExitStack() as ctx:
        sb, ps, sem, sem2 = alloc(ctx, nc, "lt")
        XS = sb("XS", [P, TOK])
        xs_tile = sb("xs_tile", [P, P])
        w_qkv = sb("w_qkv", [P, 3 * INNER])
        w_o = sb("w_o", [P, HP, P])
        w_1 = sb("w_1", [P, 2 * FF])
        w_2 = sb("w_2", [P, FT, P])
        small = sb("small", [P, NS])
        qk_gain = sb("qk_gain", [P, 2, 2, LD])
        tab = sb("tab", [P, 2, QT, 2, LD])
        tab_g = sb("tab_g", [P, 2, QT, 2, LD])
        keep = sb("keep", [P, NT])
        mask_f = sb("mask_f", [P, QT, 2 * WIN])
        mask = sb("mask", [P, QT, 2 * WIN], BF16)
        ident_b = sb("ident_b", [P, P], BF16)
        mhalf = sb("mhalf", [P, 1])
        raw = sb("raw", [P, 2, LH, LD])
        sq = sb("sq", [P, 2, CH])
        ss = sb("ss", [P, 2, LH])
        ssg = sb("ssg", [P, 2, LH])
        rn = sb("rn", [P, 2, LH])
        qn = sb("qn", [P, 2, LH, LD])
        rot_c = sb("rot_c", [P, 2, LH, LD])
        rot_s = sb("rot_s", [P, 2, LH, LD])
        q_t = sb("q_t", [P, HP, P])
        k_t = sb("k_t", [P, HP, 2, WIN + P])
        sub = sb("sub", [P, LH, 2 * WIN])
        ex = sb("ex", [P, LH, 2 * WIN])
        mx = sb("mx", [P, LH])
        dn = sb("dn", [P, LH])
        dinv = sb("dinv", [P, LH])
        ex_t = sb("ex_t", [P, HP, P])
        v_sb = sb("v_sb", [P, INNER])
        v_blk = sb("v_blk", [P, NW, HP, P])
        z_n = sb("z_n", [P, LH, LD])
        z_t = sb("z_t", [P, HP, P])
        cen = sb("cen", [P, 2, CH])
        fsq = sb("fsq", [P, 2, CH])
        ve = sb("ve", [P, 2, CH // P])
        rs = sb("rs", [P, 2, CH // P])
        xn = sb("xn", [P, 2, CH])
        hid = sb("hid", [P, 2, FT, CH])
        ln = ex[:, :, :].rearrange("p (u h) n -> p u (h n)", u=2)
        gate = sub[:, :, :].rearrange("p (u h) n -> p u (h n)", u=2)
        pP = [ps(f"pP{u}", [P, CH]) for u in range(2)]
        pT = [ps(f"pT{u}", [P, CH]) for u in range(2)]
        pS = ps("pS", [P, 2 * CH])
        pZ = ps("pZ", [P, 2 * CH])

        consts_loaded, zeros_set, consts_made, zero_stored = (sem(n) for n in ("consts_l", "zeros", "consts_m", "zero_st"))
        qkv_loaded, wo_loaded, ff_loaded, gain_loaded, tab_made = (sem(n) for n in ("qkv_l", "wo_l", "ff_l", "gain_l", "tab_m"))
        first_zero, xs_ready, tile_copied, summed = (sem(n) for n in ("first_zero", "xs_ready", "tile_copied", "summed"))
        proj, raw_done, proj_read = sem("proj"), sem("raw_done"), sem("proj_read")
        ss_done, guarded, rn_ready, qn_ready, rot_c_ready, rot_s_ready, rot_ready = (
            sem(n) for n in ("ss_done", "guarded", "rn_r", "qn_r", "rot_c_r", "rot_s_r", "rot_r"))
        qk_t, qk_evac, prev_copied = sem("qk_t"), sem("qk_evac"), sem("prev_copied")
        sc_ready, mx_ready, sub_ready, ex_ready, dn_ready, dinv_ready = (
            sem(n) for n in ("sc_r", "mx_r", "sub_r", "ex_r", "dn_r", "dinv_r"))
        ex_tr, ex_evac, pv_ready, zn_ready = sem("ex_tr"), sem("ex_evac"), sem("pv_r"), sem("zn_r")
        z_tr, z_evac, wo_ready, x_added = sem("z_tr"), sem("z_evac"), sem("wo_r"), sem("x_added")
        v_stored, v_loaded = sem("v_stored"), sem("v_loaded")
        f_mean, f_cen, f_sq, f_var, f_ve, f_rs, f_diag, f_spread, f_ln, f_xn = (
            sem2(f"f_{n}") for n in ("mean", "cen", "sq", "var", "ve", "rs", "diag", "spread", "ln", "xn"))
        f_ag, f_gate, f_hid, f_out, f_added = (sem2(f"f_{n}") for n in ("ag", "gate", "hid", "out", "added"))
        block = ctx.enter_context(nc.Block())
        FILL = 3

        def tiles(eng, l, body):
            def step(s, inside=False):
                body(s, l * NT + s, lambda lag: inside or lag <= s < NT + lag)
            for s in range(FILL + 1):
                step(s)
            with eng.Fori(FILL + 1, NT) as s:
                step(s, True)
            for s in range(NT, NT + FILL):
                step(s)

        @block.sync
        def _(sp):
            sp.dma_start(tab[:, :, :, :, :], d["c_rotary"]).then_inc(consts_loaded, 16)
            sp.dma_start(keep[:, :], d["c_keep"].to_broadcast([P, NT])).then_inc(consts_loaded, 16)
            sp.dma_start(mask_f[:, :, :], d["c_window_mask"]).then_inc(consts_loaded, 16)
            sp.wait_ge(zeros_set, 1)
            sp.dma_start(v_dram[0:WIN, :], v_blk[0:WIN, 0].rearrange("p h n -> p (h n)")).then_inc(zero_stored, 16)
            sp.wait_ge(zero_stored, 16)

            layer = lambda name, l: d[name][ds(l, 1)].rearrange("o p n -> (o p) n")

            def load_attention(l):
                sp.dma_start(qk_gain[:, :, :, :].rearrange("p a s n -> p (a s n)"),
                             layer("l_gains", l).to_broadcast([P, 4 * LD])).then_inc(gain_loaded, 16)
                sp.dma_start(w_qkv[:, :], layer("l_wqkv", l)).then_inc(qkv_loaded, 16)
                sp.dma_start(w_o[:, :, :].rearrange("p h n -> p (h n)"), layer("l_wo", l)).then_inc(wo_loaded, 16)

            load_attention(0)
            with sp.Fori(0, DEPTH) as l:
                for u in range(2):
                    sp.wait_ge(f_added[u], l * PAIRS)
                sp.dma_start(small[:, :], layer("l_small", l)).then_inc(ff_loaded, 16)
                sp.dma_start(w_1[:, :], layer("l_w1", l)).then_inc(ff_loaded, 16)
                sp.dma_start(w_2[:, :, :].rearrange("p t n -> p (t n)"), layer("l_w2", l)).then_inc(ff_loaded, 16)

                def body(s, n, on):
                    if on(1):
                        m = n - 1
                        halves = [(v_blk[c * 64:c * 64 + 64, w, :, c * 64:c * 64 + 64],
                                   v_dram[ds((s - 1) * P + w * WIN, 2 * WIN), :].rearrange("k (h c d) -> k h c d", c=2, d=LD)[:, :, c, :])
                                  for c in range(2) for w in range(NW)]
                        sp.compute_val(16 * (m + 1))
                        sp.compute_val(m)
                        sp.wait_ge(v_stored, 16 * (m + 1))
                        sp.wait_ge(pv_ready, m)
                        for dst, src in halves:
                            sp.dma_start(dst, src).then_inc(v_loaded, 16)
                    if on(0):
                        rows = v_dram[ds(WIN + s * P, P), :]
                        loaded = 16 * 2 * NW * (n - 1 if on(1) else n)
                        sp.compute_val(loaded)
                        sp.wait_ge(proj_read, 6 * (n + 1))
                        sp.wait_ge(v_loaded, loaded)
                        sp.dma_start(rows, v_sb[:, :]).then_inc(v_stored, 16)
                tiles(sp, l, body)
                sp.wait_ge(x_added, NT * (l + 1))
                load_attention((l + 1) % DEPTH)
            sp.wait_ge(gain_loaded, 16 * (DEPTH + 1))
            sp.wait_ge(qkv_loaded, 16 * (DEPTH + 1))
            sp.wait_ge(wo_loaded, 16 * (DEPTH + 1))

        @block.tensor
        def _(pe):
            pe.wait_ge(consts_made, 2)
            pe.wait_ge(first_zero, 1)
            with pe.Fori(0, DEPTH) as l:
                pe.wait_ge(qkv_loaded, 16 * (l + 1))
                pe.wait_ge(wo_loaded, 16 * (l + 1))
                pe.wait_ge(xs_ready, BATCH * (2 * l + 1))

                def body(s, n, on):
                    def project(c):
                        if not on(0):
                            return
                        pe.wait_ge(proj_read, 6 * n + max(c - 1, 0))
                        pe.matmul(pP[c % 2][:, :], xs_tile[:, :],
                                  w_qkv[:, c * CH:(c + 1) * CH], start=True, stop=True).then_inc(proj, 1)

                    def transpose_rows(bank, src, done):
                        for k in range(4):
                            mm = pe.transpose(pT[bank][:, k * P:(k + 1) * P], src(k), ident[:, :])
                        mm.then_inc(done, 1)

                    def qk_rows(side, f):
                        m = n - 1
                        pe.wait_ge(rot_ready, 2 * m + side + 1)
                        pe.wait_ge(qk_evac, 4 * m + max(2 * side + f - 1, 0))
                        transpose_rows(f, lambda k: rot_s[:, side, 8 * f + 2 * k:8 * f + 2 * k + 2, :], qk_t)

                    if on(0):
                        pe.wait_ge(tile_copied, n + l + 1)
                    project(0)
                    if on(3):
                        m = n - 3
                        pe.wait_ge(z_evac, 2 * (m + 1))
                        for h in range(HP):
                            mm = pe.matmul(pZ[:, 0:P], w_o[:, h], z_t[:, h], start=(h == 0), stop=(h == HP - 1))
                        mm.then_inc(wo_ready, 1)
                    if on(2):
                        m = n - 2
                        pe.wait_ge(z_evac, 2 * m)
                        pe.wait_ge(qk_evac, 4 * (m + 1))
                        pe.wait_ge(ex_ready, m + 1)
                        for f in range(2):
                            transpose_rows(f, lambda k: ex[:, 8 * f + 2 * k:8 * f + 2 * k + 2, :], ex_tr)
                    project(1)
                    if on(1):
                        if on(2):
                            pe.wait_ge(ex_evac, 2 * (n - 1))
                        for f in range(2):
                            qk_rows(0, f)
                    project(2)
                    if on(2):
                        m = n - 2
                        pe.wait_ge(ex_evac, 2 * (m + 1))
                        pe.wait_ge(v_loaded, 16 * 2 * NW * (m + 1))
                        pe.wait_ge(x_added, m)
                        for h in range(HP):
                            for w in range(NW):
                                mm = pe.matmul(pZ[w * WIN:(w + 1) * WIN, h * P:(h + 1) * P], ex_t[:, h, w * WIN:(w + 1) * WIN],
                                               v_blk[:, w, h], start=True, stop=True)
                        mm.then_inc(pv_ready, 1)
                    if on(1):
                        for f in range(2):
                            qk_rows(1, f)
                    project(3)
                    project(4)
                    if on(1):
                        m = n - 1
                        pe.wait_ge(qk_evac, 4 * (m + 1))
                        pe.wait_ge(sub_ready, m)
                        mt = (s - 1) % QT
                        for half in range(2):
                            pe.matmul(pS[:, half * CH:(half + 1) * CH], ident_b[:, :],
                                      bcast_mid(mask[:, ds(mt, 1), :].rearrange("p o n -> p (o n)"), HP),
                                      start=True, stop=False, skip_group_check=True)
                        for h in range(HP):
                            for w in range(NW):
                                mm = pe.matmul(pS[w * WIN:(w + 1) * WIN, h * P:(h + 1) * P], q_t[:, h, w * WIN:(w + 1) * WIN],
                                               k_t[:, h, :, w * WIN:w * WIN + 2 * WIN], start=False, stop=True,
                                               skip_group_check=True)
                        mm.then_inc(sc_ready, 1)
                    project(5)
                    if on(2):
                        m = n - 2
                        pe.wait_ge(zn_ready, m + 1)
                        for f in range(2):
                            transpose_rows(f, lambda k: z_n[:, 8 * f + 2 * k:8 * f + 2 * k + 2, :], z_tr)
                tiles(pe, l, body)

                def norm(cc, k):
                    for u in range(2):
                        pe.wait_ge(f_ln[u], k)
                        pe.matmul(pP[u][:, :], ones_mean[:, :], XS[:, ds((2 * cc + u) * CH, CH)],
                                  start=True, stop=True).then_inc(f_mean[u], 1)
                    yield
                    for u in range(2):
                        pe.wait_ge(f_sq[u], k + 1)
                        for t in range(CH // P):
                            mm = pe.matmul(pP[u][:, t:t + 1], fsq[:, u, t * P:(t + 1) * P], ones_mean[:, 0:1], start=True, stop=True)
                        mm.then_inc(f_var[u], 1)
                    yield
                    for u in range(2):
                        pe.wait_ge(f_diag[u], k + 1)
                        pe.matmul(pP[u][:, :], ones[:, :], fsq[:, u], start=True, stop=True).then_inc(f_spread[u], 1)
                    yield

                def mlp(cc, k, ahead):
                    next(ahead, None)
                    for t in range(FT):
                        for u in range(2):
                            pe.wait_ge(f_xn[u], k + 1)
                            pe.wait_ge(f_hid[u], FT * k + t)
                            pe.matmul(pT[u][0:FROWS[t], :], w_1[:, t * P:t * P + FROWS[t]], xn[:, u], start=True, stop=True)
                            pe.matmul(pS[0:FROWS[t], u * CH:(u + 1) * CH], w_1[:, FF + t * P:FF + t * P + FROWS[t]], xn[:, u],
                                      start=True, stop=True).then_inc(f_ag[u], 1)
                        next(ahead, None)
                    for u in range(2):
                        pe.wait_ge(f_hid[u], FT * (k + 1))
                        for t in range(FT):
                            mm = pe.matmul(pZ[:, u * CH:(u + 1) * CH], w_2[0:FROWS[t], t], hid[0:FROWS[t], u, t],
                                           start=(t == 0), stop=(t == FT - 1))
                        mm.then_inc(f_out[u], 1)

                pe.wait_ge(ff_loaded, 48 * (l + 1))
                pe.wait_ge(xs_ready, BATCH * (2 * l + 2))
                for _ in norm(0, l * PAIRS):
                    pass
                with pe.Fori(0, PAIRS - 1) as cc:
                    mlp(cc, l * PAIRS + cc, norm(cc + 1, l * PAIRS + cc + 1))
                mlp(PAIRS - 1, l * PAIRS + PAIRS - 1, iter(()))

        @block.scalar
        def _(act):
            act.wait_ge(first_zero, 1)
            act.wait_ge(zeros_set, 3)
            with act.Fori(0, DEPTH) as l:
                act.wait_ge(xs_ready, BATCH * (2 * l + 1))
                act.activation(xs_tile[:, :], XS[:, 0:P], ACT.Copy).then_inc(tile_copied, 1)

                def body(s, n, on):
                    def read_chunk(c):
                        if not on(0):
                            return
                        act.wait_ge(proj, 6 * n + c + 1)
                        if c < 4:
                            act.wait_ge(qn_ready, 2 * n - (1 if on(1) and c < 2 else 0))
                            dst = raw[:, c // 2, 8 * (c % 2):8 * (c % 2) + 8, :].rearrange("p h n -> p (h n)")
                            act.activation(dst, pP[c % 2][:, :], ACT.Copy)
                            act.wait_ge(ss_done, 4 * n + max(c - 1, 0))
                            act.activation(sq[:, c % 2], pP[c % 2][:, :], ACT.Square).then_inc(proj_read, 1)
                        else:
                            act.wait_ge(v_stored, 16 * n)
                            act.activation(v_sb[:, (c - 4) * CH:(c - 3) * CH], pP[c % 2][:, :], ACT.Copy).then_inc(proj_read, 1)

                    read_chunk(0)
                    if on(2):
                        m = n - 2
                        act.wait_ge(pv_ready, m)
                        for f in range(2):
                            act.wait_ge(ex_tr, 2 * m + f + 1)
                            act.activation(ex_t[:, 4 * f:4 * f + 4].rearrange("p h n -> p (h n)"), pT[f][:, :], ACT.Copy).then_inc(ex_evac, 1)
                    read_chunk(1)
                    if on(1):
                        m = n - 1
                        act.wait_ge(sc_ready, m)
                        for f in range(2):
                            act.wait_ge(qk_t, 4 * m + f + 1)
                            act.activation(q_t[:, 4 * f:4 * f + 4].rearrange("p h n -> p (h n)"), pT[f][:, :], ACT.Copy).then_inc(qk_evac, 1)
                        act.activation(k_t[:, :, :, 0:WIN].rearrange("p h c n -> p (h c) n"),
                                       k_t[:, :, :, P:P + WIN].rearrange("p h c n -> p (h c) n"), ACT.Copy,
                                       scale=keep[:, ds(s - 1, 1)]).then_inc(prev_copied, 1)
                    read_chunk(2)
                    if on(1):
                        act.wait_ge(prev_copied, m + 1)
                        for f in range(2):
                            act.wait_ge(qk_t, 4 * m + 2 + f + 1)
                            for c in range(2):
                                mm = act.activation(k_t[c * 64:c * 64 + 64, 4 * f:4 * f + 4, c, WIN:WIN + P],
                                                    pT[f][c * 64:c * 64 + 64, :].rearrange("p (h n) -> p h n", n=P), ACT.Copy)
                            mm.then_inc(qk_evac, 1)
                    read_chunk(3)
                    read_chunk(4)
                    read_chunk(5)
                    if on(0):
                        act.activation(xs_tile[:, :], XS[:, ds((s + 1) % NT * P, P)], ACT.Copy).then_inc(tile_copied, 1)
                    if on(2):
                        m = n - 2
                        act.wait_ge(wo_ready, m)
                        for f in range(2):
                            act.wait_ge(z_tr, 2 * m + f + 1)
                            act.activation(z_t[:, 4 * f:4 * f + 4].rearrange("p h n -> p (h n)"), pT[f][:, :], ACT.Copy).then_inc(z_evac, 1)
                    if on(1):
                        m = n - 1
                        act.wait_ge(sub_ready, m + 1)
                        act.wait_ge(dn_ready, m)
                        act.activation(ex[:, :, :], sub[:, :, :], ACT.Exp).then_inc(ex_ready, 1)
                tiles(act, l, body)

                def norm(cc, k):
                    for u in range(2):
                        act.wait_ge(f_cen[u], k + 1)
                        act.activation(fsq[:, u], cen[:, u], ACT.Square).then_inc(f_sq[u], 1)
                    yield
                    for u in range(2):
                        act.wait_ge(f_ln[u], k + 1)
                        act.wait_ge(f_ag[u], FT * k)
                        act.activation(xn[:, u], ln[:, u], ACT.Identity, bias=small[:, 8:9]).then_inc(f_xn[u], 1)
                    yield

                def mlp(cc, k, ahead):
                    next(ahead, None)
                    for t in range(FT):
                        for u in range(2):
                            R = FROWS[t]
                            act.wait_ge(f_hid[u], FT * k + t)
                            act.wait_ge(f_ag[u], FT * k + t + 1)
                            act.activation(gate[0:R, u], pS[0:R, u * CH:(u + 1) * CH], ACT.Gelu,
                                           bias=small[0:R, 3 + t:4 + t]).then_inc(f_gate[u], 1)
                    next(ahead, None)

                act.wait_ge(ff_loaded, 48 * (l + 1))
                for _ in norm(0, l * PAIRS):
                    pass
                with act.Fori(0, PAIRS - 1) as cc:
                    mlp(cc, l * PAIRS + cc, norm(cc + 1, l * PAIRS + cc + 1))
                mlp(PAIRS - 1, l * PAIRS + PAIRS - 1, iter(()))

        @block.gpsimd
        def _(pool):
            pool.memset(v_blk[:, :, :, :], 0.0).then_inc(zeros_set, 1)
            pool.memset(k_t[:, :, :, :], 0.0).then_inc(zeros_set, 1)
            pool.memset(mhalf[:, :], -0.5).then_inc(zeros_set, 1)
            pool.wait_ge(consts_loaded, 48)
            pool.tensor_copy(mask[:, :, :], mask_f[:, :, :]).then_inc(consts_made, 1)
            pool.tensor_copy(ident_b[:, :], ident[:, :]).then_inc(consts_made, 1)
            pool.wait_ge(zeros_set, 3)

            def make_tables(l):
                pool.wait_ge(gain_loaded, 16 * (l + 1))
                for a in range(2):
                    mm = pool.tensor_tensor(tab_g[:, a].rearrange("p t s n -> p t (s n)"), tab[:, a].rearrange("p t s n -> p t (s n)"),
                                            bcast_mid(qk_gain[:, a].rearrange("p s n -> p (s n)"), QT), ALU.mult)
                mm.then_inc(tab_made, 1)

            make_tables(0)
            with pool.Fori(0, DEPTH) as l:

                def body(s, n, on):
                    if not on(0):
                        return
                    for side in range(2):
                        pool.wait_ge(guarded, 2 * n + side + 1)
                        pool.tensor_tensor(rn[:, side], ssg[:, side], mhalf[:, :].to_broadcast([P, LH]), ALU.pow).then_inc(rn_ready, 1)
                        pool.wait_ge(qn_ready, 2 * n + side + 1)
                        t = s % QT
                        tb = tab_g[:, 0, ds(t, 1), side, :].rearrange("p o n -> p (o n)")
                        pool.tensor_tensor(rot_c[:, side], qn[:, side], bcast_mid(tb, LH), ALU.mult).then_inc(rot_c_ready, 1)
                pool.wait_ge(tab_made, l + 1)
                tiles(pool, l, body)
                with pool.Fori(0, NCH // 2) as cc:
                    k = l * (NCH // 2) + cc
                    for u in range(2):
                        pool.wait_ge(f_ve[u], k + 1)
                        pool.tensor_tensor(rs[:, u], ve[:, u], mhalf[:, :].to_broadcast([P, CH // P]), ALU.pow).then_inc(f_rs[u], 1)
                pool.wait_ge(x_added, NT * (l + 1))
                make_tables(l + 1)

        @block.vector
        def _(dve):
            dve.wait_ge(consts_made, 2)
            dve.memset(XS[64:P, 0:TOK:SEQ], 0.0).then_inc(first_zero, 1)

            def shift(b):
                c = b * SEQ
                dve.tensor_scalar(XS[0:64, ds(c, SEQ)], X[0:64, ds(c, SEQ)], 1.0, None, ALU.mult)
                dve.tensor_scalar(XS[64:P, ds(c + 1, SEQ - 1)], X[64:P, ds(c, SEQ - 1)], 1.0, None, ALU.mult).then_inc(xs_ready, 1)

            for b in range(BATCH):
                shift(b)
            with dve.Fori(0, DEPTH) as l:
                dve.wait_ge(tab_made, l + 1)

                def body(s, n, on):
                    t = s % QT

                    def sum_squares(c):
                        if not on(0):
                            return
                        dve.wait_ge(proj_read, 6 * n + c + 1)
                        side, half = c // 2, c % 2
                        dve.tensor_reduce(ss[:, side, 8 * half:8 * half + 8], sq[:, half].rearrange("p (h n) -> p h n", n=LD),
                                          AX.X, ALU.add).then_inc(ss_done, 1)

                    def guard(side):
                        if on(0):
                            dve.wait_ge(ss_done, 4 * n + 2 * side + 2)
                            dve.tensor_scalar(ssg[:, side], ss[:, side], L2_MIN, None, ALU.max).then_inc(guarded, 1)

                    def normalise(side):
                        if on(0):
                            dve.wait_ge(rn_ready, 2 * n + side + 1)
                            dve.tensor_tensor(qn[:, side], raw[:, side], bcast_last(rn[:, side], LD), ALU.mult).then_inc(qn_ready, 1)

                    def rotate_sine(side, m, t):
                        dve.wait_ge(qn_ready, 2 * m + side + 1)
                        dve.wait_ge(qk_t, 4 * m - (2 if side == 0 and on(1) else 0))
                        for h in range(2):
                            tb = tab_g[:, 1, ds(t, 1), side, 32 * h:32 * h + 32].rearrange("p o n -> p (o n)")
                            mm = dve.tensor_tensor(rot_s[:, side, :, 32 * h:32 * h + 32], qn[:, side, :, 32 - 32 * h:64 - 32 * h],
                                                   bcast_mid(tb, LH), ALU.mult)
                        mm.then_inc(rot_s_ready, 1)

                    def rotate_sum(side, m):
                        dve.wait_ge(rot_s_ready, 2 * m + side + 1)
                        dve.wait_ge(rot_c_ready, 2 * m + side + 1)
                        dve.tensor_tensor(rot_s[:, side], rot_s[:, side], rot_c[:, side], ALU.add).then_inc(rot_ready, 1)

                    if on(1):
                        rotate_sine(1, n - 1, (s - 1) % QT)
                    sum_squares(0)
                    if on(3):
                        m = n - 3
                        dve.wait_ge(wo_ready, m + 1)
                        cols = ds((s - 3) * P, P)
                        dve.tensor_tensor(X[:, cols], X[:, cols], pZ[:, 0:P], ALU.add).then_inc(x_added, 1)
                    if on(1):
                        rotate_sum(1, n - 1)
                    sum_squares(1)
                    guard(0)
                    if on(2):
                        m = n - 2
                        dve.wait_ge(ex_ready, m + 1)
                        dve.tensor_reduce(dn[:, :], ex[:, :, :], AX.X, ALU.add).then_inc(dn_ready, 1)
                        dve.wait_ge(dn_ready, m + 1)
                        dve.reciprocal(dinv[:, :], dn[:, :]).then_inc(dinv_ready, 1)
                    sum_squares(2)
                    if on(2):
                        m = n - 2
                        dve.wait_ge(pv_ready, m + 1)
                        dve.wait_ge(dinv_ready, m + 1)
                        dve.wait_ge(z_tr, 2 * m)
                        dve.tensor_tensor(z_n[:, :, :], pZ[:, :].rearrange("p (h n) -> p h n", n=LD),
                                          bcast_last(dinv[:, :], LD), ALU.mult).then_inc(zn_ready, 1)
                    normalise(0)
                    if on(0):
                        rotate_sine(0, n, t)
                    sum_squares(3)
                    guard(1)
                    if on(0):
                        rotate_sum(0, n)
                    if on(1):
                        m = n - 1
                        dve.wait_ge(sc_ready, m + 1)
                        sc = pS[:, :].rearrange("p (h n) -> p h n", n=2 * WIN)
                        dve.tensor_reduce(mx[:, :], sc, AX.X, ALU.max).then_inc(mx_ready, 1)
                        dve.wait_ge(mx_ready, m + 1)
                        dve.wait_ge(ex_ready, m)
                        dve.tensor_tensor(sub[:, :, :], sc, bcast_last(mx[:, :], 2 * WIN), ALU.subtract).then_inc(sub_ready, 1)
                    normalise(1)
                    if not on(0):
                        b = s - NT
                        dve.wait_ge(tile_copied, (NT + 1) * (l + 1))
                        dve.wait_ge(x_added, NT * l + QT * (b + 1))
                        shift(b)
                tiles(dve, l, body)
                dve.wait_ge(x_added, NT * (l + 1))
                shift(BATCH - 1)

                def norm(cc, k):
                    for u in range(2):
                        cols = ds((2 * cc + u) * CH, CH)
                        dve.wait_ge(f_mean[u], k + 1)
                        dve.tensor_tensor(cen[:, u], XS[:, cols], pP[u][:, :], ALU.subtract).then_inc(f_cen[u], 1)
                    yield
                    for u in range(2):
                        dve.wait_ge(f_var[u], k + 1)
                        dve.tensor_scalar(ve[:, u], pP[u][:, 0:CH // P], LN_EPS, None, ALU.add).then_inc(f_ve[u], 1)
                    yield
                    for u in range(2):
                        dve.wait_ge(f_rs[u], k + 1)
                        for t in range(CH // P):
                            mm = dve.tensor_scalar(fsq[:, u, t * P:(t + 1) * P], ident[:, :], rs[:, u, t:t + 1], None, ALU.mult)
                        mm.then_inc(f_diag[u], 1)
                    yield
                    for u in range(2):
                        dve.wait_ge(f_spread[u], k + 1)
                        dve.scalar_tensor_tensor(out=ln[:, u], in0=cen[:, u], scalar=small[:, 7:8], in1=pP[u][:, :],
                                                 op0=ALU.mult, op1=ALU.mult).then_inc(f_ln[u], 1)
                    yield

                def mlp(cc, k, ahead):
                    next(ahead, None)
                    for t in range(FT):
                        for u in range(2):
                            R = FROWS[t]
                            dve.wait_ge(f_gate[u], FT * k + t + 1)
                            dve.scalar_tensor_tensor(out=hid[0:R, u, t], in0=pT[u][0:R, :], scalar=small[0:R, t:t + 1], in1=gate[0:R, u],
                                                     op0=ALU.add, op1=ALU.mult).then_inc(f_hid[u], 1)
                        next(ahead, None)
                        if t == 0:
                            next(ahead, None)
                    for u in range(2):
                        cols = ds((2 * cc + u) * CH, CH)
                        dve.wait_ge(f_out[u], k + 1)
                        dve.scalar_tensor_tensor(out=X[:, cols], in0=pZ[:, u * CH:(u + 1) * CH], scalar=small[:, 6:7],
                                                 in1=X[:, cols], op0=ALU.add, op1=ALU.add).then_inc(f_added[u], 1)
                    for u in range(2):
                        dve.wait_ge(f_added[u], k + 1)
                    shift(cc)

                dve.wait_ge(ff_loaded, 48 * (l + 1))
                for _ in norm(0, l * PAIRS):
                    pass
                with dve.Fori(0, PAIRS - 1) as cc:
                    mlp(cc, l * PAIRS + cc, norm(cc + 1, l * PAIRS + cc + 1))
                mlp(PAIRS - 1, l * PAIRS + PAIRS - 1, iter(()))

            dve.tensor_tensor(XR[:, :], XR[:, :], X[:, :], ALU.add).then_inc(summed, 1)
            dve.wait_ge(summed, 1)


def rotary_constants():
    f32 = np.float32
    half = np.arange(0, LD, 2, dtype=f32)
    inv_freq = f32(1.0) / f32(10000.0) ** (half / f32(LD))
    t = np.arange(SEQ, dtype=f32)
    freqs = t[:, None] * inv_freq[None, :]
    base = (half + f32(0.4 * LD)) / f32(1.4 * LD)
    power = (t - f32(SEQ // 2)) / f32(WIN // 2)
    scale = base[None, :] ** power[:, None]
    out = np.zeros((2, 2, SEQ, LD), f32)
    for side, sc in enumerate((scale * f32(8.0), f32(1.0) / scale)):
        cos, sin = np.cos(freqs) * sc, np.sin(freqs) * sc
        out[0, side] = np.concatenate([cos, cos], -1)
        out[1, side] = np.concatenate([-sin, sin], -1)
    return np.ascontiguousarray(out.reshape(2, 2, QT, P, LD).transpose(3, 0, 2, 1, 4))


def window_mask():
    i = (np.arange(P) % WIN)[:, None]
    j = np.arange(2 * WIN)[None, :]
    seen = np.where(j < WIN, i <= j, i >= j - WIN)
    m = np.repeat(seen[:, None, :], QT, 1)
    m[0:WIN, 0, 0:WIN] = False
    return np.where(m, 0.0, NEG).astype(np.float32)


def swap_halves(a):
    return np.concatenate([a[..., LD // 2:], a[..., :LD // 2]], -1)


def layout_more(f):
    a = {}
    a["l_wqkv"] = f["L0_ffn_Wqkv"]
    a["l_wo"] = f["L0_ffn_Wo"].reshape(DEPTH, HP, P, P).transpose(0, 2, 1, 3).reshape(DEPTH, P, HP * P)
    a["l_w1"] = f["L0_ffn_W1"]
    w2 = np.zeros((DEPTH, FT * P, P), np.float32)
    w2[:, 0:FF] = f["L0_ffn_W2"]
    a["l_w2"] = w2.reshape(DEPTH, FT, P, P).transpose(0, 2, 1, 3).reshape(DEPTH, P, FT * P)
    small = np.zeros((DEPTH, P, NS), np.float32)
    for t in range(FT):
        small[:, 0:FROWS[t], t] = f["L0_ffn_b1"][:, t * P:t * P + FROWS[t]]
        small[:, 0:FROWS[t], 3 + t] = f["L0_ffn_b1"][:, FF + t * P:FF + t * P + FROWS[t]]
    small[:, :, 6] = f["L0_ffn_b2"]
    small[:, :, 7] = f["L0_ffn_ln_g"]
    small[:, :, 8] = f["L0_ffn_ln_b"]
    a["l_small"] = small
    q, k = f["L0_ffn_q_scale"], f["L0_ffn_k_scale"]
    a["l_gains"] = np.stack([q, k, swap_halves(q), swap_halves(k)], 1).reshape(DEPTH, 1, 4 * LD)
    a["c_rotary"] = rotary_constants()
    a["c_window_mask"] = window_mask()
    a["c_keep"] = (np.arange(NT) % QT != 0).astype(np.float32).reshape(1, NT)
    return a


FI = 352
FIT = 3
FIROWS = [P, P, FI - 2 * P]
QB = 16
FP4_MAX, FP4_MIN_SCALE = 6.0, 1e-12
BOUND_4 = 5.0
BOUNDS_2 = (3.5, 2.5)
BOUNDS_1 = (1.75, 1.25, 0.75, 0.25)
FP4_SUMS = 1 + len(BOUNDS_2) + 1 + len(BOUNDS_1)


class Fp4Buffers:

    def __init__(q, sb, sem2, width):
        q.top = sb("q_top", [P, 2, width // QB])
        q.scale = sb("q_scale", [P, 2, width // QB])
        q.half_scale = sb("q_half_scale", [P, 2, width // QB])
        q.inv = sb("q_inv", [P, 2, width // QB])
        q.xn = sb("q_xn", [P, 2, width])
        q.mag = sb("q_mag", [P, 2, width])
        q.sign = sb("q_sign", [P, 2, width])
        q.unit = sb("q_unit", [P, 2, width])
        q.steps = sb("q_steps", [P, 2, width])
        q.top_r, q.scale_r, q.half_r, q.inv_r = (sem2(f"q_{n}") for n in ("top_r", "scale_r", "half_r", "inv_r"))
        q.xn_r, q.mag_r, q.unit_r, q.sums, q.done = (sem2(f"q_{n}") for n in ("xn_r", "mag_r", "unit_r", "sums", "done"))


def blocks(ap):
    return ap.rearrange("p (b n) -> p b n", n=QB)


def fp4_vector(dve, q, k, lanes, wait_src, src):
    for u in lanes:
        wait_src(u)
        dve.tensor_reduce(q.top[:, u], blocks(src(u)), AX.X, ALU.max, apply_absolute_value=True).then_inc(q.top_r[u], 1)
    for u in lanes:
        dve.wait_ge(q.top_r[u], k + 1)
        dve.tensor_scalar(q.scale[:, u], q.top[:, u], 1.0 / FP4_MAX, FP4_MIN_SCALE, ALU.mult, ALU.max).then_inc(q.scale_r[u], 1)
    for u in lanes:
        dve.wait_ge(q.scale_r[u], k + 1)
        dve.reciprocal(q.inv[:, u], q.scale[:, u]).then_inc(q.inv_r[u], 1)
        dve.wait_ge(q.unit_r[u], k)
        dve.tensor_scalar(q.half_scale[:, u], q.scale[:, u], 0.5, None, ALU.mult).then_inc(q.half_r[u], 1)
    for u in lanes:
        dve.wait_ge(q.inv_r[u], k + 1)
        dve.tensor_tensor(blocks(q.xn[:, u]), blocks(src(u)), bcast_last(q.inv[:, u], QB), ALU.mult).then_inc(q.xn_r[u], 1)
    n = 0
    for u in lanes:
        dve.wait_ge(q.mag_r[u], k + 1)
        dve.tensor_scalar(q.steps[:, u], q.mag[:, u], BOUND_4, 2.0, ALU.is_gt, ALU.mult).then_inc(q.sums[u], 1)
    for bounds, last in ((BOUNDS_2, False), (BOUNDS_1, True)):
        for bound in bounds:
            n += 1
            for u in lanes:
                dve.wait_ge(q.sums[u], FP4_SUMS * k + n)
                dve.scalar_tensor_tensor(out=q.steps[:, u], in0=q.mag[:, u], scalar=bound, in1=q.steps[:, u],
                                         op0=ALU.is_gt, op1=ALU.add).then_inc(q.sums[u], 1)
        if not last:
            n += 1
            for u in lanes:
                dve.wait_ge(q.sums[u], FP4_SUMS * k + n)
                dve.tensor_scalar(q.steps[:, u], q.steps[:, u], 2.0, None, ALU.mult).then_inc(q.sums[u], 1)


def fp4_scalar(act, q, k, lanes):
    for u in lanes:
        act.wait_ge(q.xn_r[u], k + 1)
        act.wait_ge(q.done[u], k)
        act.activation(q.mag[:, u], q.xn[:, u], ACT.Abs)
        act.activation(q.sign[:, u], q.xn[:, u], ACT.Sign).then_inc(q.mag_r[u], 1)


def fp4_gpsimd(pool, q, k, lanes, dst, wait_dst):
    for u in lanes:
        pool.wait_ge(q.half_r[u], k + 1)
        pool.wait_ge(q.mag_r[u], k + 1)
        pool.tensor_tensor(blocks(q.unit[:, u]), blocks(q.sign[:, u]), bcast_last(q.half_scale[:, u], QB),
                           ALU.mult).then_inc(q.unit_r[u], 1)
    for u in lanes:
        pool.wait_ge(q.unit_r[u], k + 1)
        wait_dst(u)
        pool.wait_ge(q.sums[u], FP4_SUMS * (k + 1))
        pool.tensor_tensor(dst(u), q.steps[:, u], q.unit[:, u], ALU.mult).then_inc(q.done[u], 1)


def fp4_mlp(nc, d, XR, ident, ones, ones_mean):
    with ExitStack() as outer:
        w_gate = outer.enter_context(nc.sbuf_tensor("fp_w_gate", [P, FIT * P], F32))
        w_up = outer.enter_context(nc.sbuf_tensor("fp_w_up", [P, FIT * P], F32))
        w_down = outer.enter_context(nc.sbuf_tensor("fp_w_down", [P, FIT, P], F32))
        XN = outer.enter_context(nc.sbuf_tensor("fp_XN", [P, TOK], F32))
        quantise_weights(nc, d, ident, w_gate, w_up, w_down)
        layer_norm_all(nc, "fp_ln", XR, XN, ident, ones, ones_mean)
        quantise_tokens(nc, XN, ident)
        gated_mlp(nc, XR, XN, ident, w_gate, w_up, w_down)


def quantise_weights(nc, d, ident, w_gate, w_up, w_down):
    with ExitStack() as ctx:
        sb, ps, sem, sem2 = alloc(ctx, nc, "fw")
        W = FIT * P
        raw = sb("raw", [P, 3, W])
        deq = sb("deq", [P, 3, W])
        pT = [ps(f"pT{i}", [P, CH]) for i in range(3)]
        loaded, transposed, evacuated = sem("loaded"), sem("transposed"), sem("evacuated")
        q = Fp4Buffers(sb, sem2, W)
        block = ctx.enter_context(nc.Block())

        @block.sync
        def _(sp):
            for i, name in enumerate(("f_gate", "f_up", "f_down")):
                sp.dma_start(raw[:, i], d[name]).then_inc(loaded, 16)

        @block.tensor
        def _(pe):
            for i in range(3):
                u, k = i % 2, i // 2
                pe.wait_ge(q.done[u], k + 1)
                for t in range(FIT):
                    mm = pe.transpose(pT[i][:, t * P:(t + 1) * P], deq[:, i, t * P:(t + 1) * P], ident[:, :])
                mm.then_inc(transposed, 1)

        @block.vector
        def _(dve):
            dve.wait_ge(loaded, 48)
            fp4_vector(dve, q, 0, (0, 1), lambda u: None, lambda u: raw[:, u])
            dve.wait_ge(q.done[0], 1)
            fp4_vector(dve, q, 1, (0,), lambda u: None, lambda u: raw[:, 2])

        @block.scalar
        def _(act):
            fp4_scalar(act, q, 0, (0, 1))
            fp4_scalar(act, q, 1, (0,))
            for i, dst in enumerate((w_gate[:, :], w_up[:, :], w_down[:, :, :].rearrange("p t n -> p (t n)"))):
                act.wait_ge(transposed, i + 1)
                act.activation(dst, pT[i][:, 0:W], ACT.Copy).then_inc(evacuated, 1)
            act.wait_ge(evacuated, 3)

        @block.gpsimd
        def _(pool):
            fp4_gpsimd(pool, q, 0, (0, 1), lambda u: deq[:, u], lambda u: None)
            fp4_gpsimd(pool, q, 1, (0,), lambda u: deq[:, 2], lambda u: None)


def quantise_tokens(nc, XN, ident):
    with ExitStack() as ctx:
        sb, ps, sem, sem2 = alloc(ctx, nc, "fx")
        x_in = sb("x_in", [P, 2, CH])
        deq = sb("deq", [P, 2, CH])
        pX = [ps(f"pX{u}", [P, CH]) for u in range(2)]
        pB = [ps(f"pB{u}", [P, CH]) for u in range(2)]
        copied, x_t, back_t, back = sem2("copied"), sem2("x_t"), sem2("back_t"), sem2("back")
        q = Fp4Buffers(sb, sem2, CH)
        block = ctx.enter_context(nc.Block())

        @block.tensor
        def _(pe):
            with pe.Fori(0, NCH // 2) as cc:
                for u in range(2):
                    pe.wait_ge(copied[u], cc + 1)
                    pe.wait_ge(q.xn_r[u], cc)
                    for t in range(CH // P):
                        mm = pe.transpose(pX[u][:, t * P:(t + 1) * P], x_in[:, u, t * P:(t + 1) * P], ident[:, :])
                    mm.then_inc(x_t[u], 1)
                for u in range(2):
                    pe.wait_ge(back[u], cc)
                    pe.wait_ge(q.done[u], cc + 1)
                    for t in range(CH // P):
                        mm = pe.transpose(pB[u][:, t * P:(t + 1) * P], deq[:, u, t * P:(t + 1) * P], ident[:, :])
                    mm.then_inc(back_t[u], 1)

        @block.vector
        def _(dve):
            with dve.Fori(0, NCH // 2) as cc:
                fp4_vector(dve, q, cc, (0, 1), lambda u: dve.wait_ge(x_t[u], cc + 1), lambda u: pX[u][:, :])
                for u in range(2):
                    dve.wait_ge(back_t[u], cc + 1)
                    dve.tensor_scalar(XN[:, ds((2 * cc + u) * CH, CH)], pB[u][:, :], 1.0, None, ALU.mult).then_inc(back[u], 1)

        @block.scalar
        def _(act):
            with act.Fori(0, NCH // 2) as cc:
                for u in range(2):
                    act.wait_ge(x_t[u], cc)
                    act.activation(x_in[:, u], XN[:, ds((2 * cc + u) * CH, CH)], ACT.Copy).then_inc(copied[u], 1)
                fp4_scalar(act, q, cc, (0, 1))

        @block.gpsimd
        def _(pool):
            with pool.Fori(0, NCH // 2) as cc:
                fp4_gpsimd(pool, q, cc, (0, 1), lambda u: deq[:, u], lambda u: pool.wait_ge(back_t[u], cc))


def gated_mlp(nc, XR, XQ, ident, w_gate, w_up, w_down):
    with ExitStack() as ctx:
        sb, ps, sem, sem2 = alloc(ctx, nc, "fm")
        x_tile = sb("x_tile", [P, 2, P])
        silu = sb("silu", [P, 2, FI])
        h = sb("h", [P, 2, FI])
        deq = sb("deq", [P, 2, FI])
        hid = sb("hid", [P, FIT, 2, P])
        pG = [ps(f"pG{u}", [P, CH]) for u in range(2)]
        pU = [ps(f"pU{u}", [P, CH]) for u in range(2)]
        pT = [ps(f"pT{u}", [P, CH]) for u in range(2)]
        pO = ps("pO", [P, CH])
        tiles_copied, gate_up, silu_r, h_r, h_t, hid_r = (sem2(n) for n in ("tiles", "gate_up", "silu_r", "h_r", "h_t", "hid_r"))
        out_r, added = sem("out_r"), sem("added")
        q = Fp4Buffers(sb, sem2, FI)
        block = ctx.enter_context(nc.Block())
        N = NT // 2

        def pairs(eng, body):
            body(0, True, False)
            with eng.Fori(1, N - 1) as i:
                body(i, False, False)
            body(N - 1, False, True)

        @block.tensor
        def _(pe):
            def project(i):
                for u in range(2):
                    pe.wait_ge(tiles_copied[u], i + 1)
                    pe.wait_ge(h_r[u], i)
                    pe.matmul(pG[u][:, 0:FI], x_tile[:, u], w_gate[:, 0:FI], start=True, stop=True)
                    pe.matmul(pU[u][:, 0:FI], x_tile[:, u], w_up[:, 0:FI], start=True, stop=True).then_inc(gate_up[u], 1)
            project(0)

            def body(i, first, last):
                if not last:
                    project(i + 1)
                for u in range(2):
                    pe.wait_ge(q.done[u], i + 1)
                    pe.wait_ge(hid_r[u], i)
                    for t in range(FIT):
                        R = FIROWS[t]
                        mm = pe.transpose(pT[u][0:R, t * P:(t + 1) * P], deq[:, u, t * P:t * P + R], ident[:, :])
                    mm.then_inc(h_t[u], 1)
                for u in range(2):
                    pe.wait_ge(hid_r[u], i + 1)
                pe.wait_ge(added, i)
                for t in range(FIT):
                    R = FIROWS[t]
                    mm = pe.matmul(pO[:, 0:2 * P], w_down[0:R, t], hid[0:R, t].rearrange("p u n -> p (u n)"),
                                   start=(t == 0), stop=(t == FIT - 1))
                mm.then_inc(out_r, 1)
            pairs(pe, body)

        @block.scalar
        def _(act):
            def copy_tiles(i):
                for u in range(2):
                    act.wait_ge(gate_up[u], i)
                    act.activation(x_tile[:, u], XQ[:, ds((2 * i + u) * P, P)], ACT.Copy).then_inc(tiles_copied[u], 1)

            def gates(i):
                for u in range(2):
                    act.wait_ge(gate_up[u], i + 1)
                    act.wait_ge(h_r[u], i)
                    act.activation(silu[:, u], pG[u][:, 0:FI], ACT.Silu).then_inc(silu_r[u], 1)
            copy_tiles(0)
            gates(0)

            def body(i, first, last):
                if not last:
                    copy_tiles(i + 1)
                fp4_scalar(act, q, i, (0, 1))
                if not last:
                    gates(i + 1)
                act.wait_ge(out_r, i)
                for u in range(2):
                    act.wait_ge(h_t[u], i + 1)
                    for t in range(FIT):
                        R = FIROWS[t]
                        mm = act.activation(hid[0:R, t, u], pT[u][0:R, t * P:(t + 1) * P], ACT.Copy)
                    mm.then_inc(hid_r[u], 1)
            pairs(act, body)

        @block.gpsimd
        def _(pool):
            pairs(pool, lambda i, first, last: fp4_gpsimd(pool, q, i, (0, 1), lambda u: deq[:, u],
                                                          lambda u: pool.wait_ge(h_t[u], i)))

        @block.vector
        def _(dve):
            def add_out(i):
                cols = ds(2 * i * P, 2 * P)
                dve.wait_ge(out_r, i + 1)
                dve.tensor_tensor(XR[:, cols], XR[:, cols], pO[:, 0:2 * P], ALU.add).then_inc(added, 1)

            def body(i, first, last):
                for u in range(2):
                    dve.wait_ge(silu_r[u], i + 1)
                    dve.tensor_tensor(h[:, u], silu[:, u], pU[u][:, 0:FI], ALU.mult).then_inc(h_r[u], 1)
                fp4_vector(dve, q, i, (0, 1), lambda u: dve.wait_ge(h_r[u], i + 1), lambda u: h[:, u])
                if not first:
                    add_out(i - 1)
                if last:
                    add_out(i)
            pairs(dve, body)


def layout_fp4(f):
    a = {}
    for name, src in (("f_gate", "L1_ffn_w_gate"), ("f_up", "L1_ffn_w_up")):
        w = np.zeros((FIT * P, P), np.float32)
        w[0:FI] = f[src]
        a[name] = w.reshape(FIT, P, P).transpose(1, 0, 2).reshape(P, FIT * P)
    w = np.zeros((P, FIT * P), np.float32)
    w[:, 0:FI] = f["L1_ffn_w_down"]
    a["f_down"] = w
    return a


def host_constants():
    c = {}
    c["c_ident"] = np.eye(P, dtype=np.float32)
    c["c_ones"] = np.ones((P, P), np.float32)
    c["c_ones_mean"] = np.full((P, P), 1.0 / P, np.float32)
    heads = np.arange(P) // HD
    c["c_head_mean"] = np.where(heads[:, None] == np.arange(HEADS)[None, :], 1.0 / HD, 0.0).astype(np.float32)
    spread = np.zeros((P, P), np.float32)
    for j in range(GRP):
        spread[32 * j + HD, 32 * j:32 * j + 32] = 1.0
    c["c_spread_den"] = spread
    k, q = np.arange(P)[:, None], np.arange(P)[None, :]
    c["c_causal"] = np.stack([np.where(k > q, NEG, 0.0), np.where(q > k, NEG, 0.0)], 1).astype(np.float32)
    return c


def pad_heads(wo_t):
    out = np.zeros((GRP, 32, NGRP, P), wo_t.dtype)
    out[:, 0:HD] = wo_t.reshape(NGRP, GRP, HD, P).transpose(1, 2, 0, 3)
    return out.reshape(P, NGRP, P)


def build(nc, d, out_t):
    with ExitStack() as ctx:
        XR = ctx.enter_context(nc.sbuf_tensor("XR", [P, TOK], F32))
        ident = ctx.enter_context(nc.sbuf_tensor("ident", [P, P], F32))
        ones_mean = ctx.enter_context(nc.sbuf_tensor("ones_mean", [P, P], F32))
        ones = ctx.enter_context(nc.sbuf_tensor("ones", [P, P], F32))
        q_parts = nc.dram_tensor("q_parts", (PARTS, P, TOK), BF16, kind="Internal").ap()
        k_parts = nc.dram_tensor("k_parts", (PARTS, P, TOK), BF16, kind="Internal").ap()
        v_rows = nc.dram_tensor("v_rows", (TOK, P), F32, kind="Internal").ap()
        load_residual(nc, d, XR, ident, ones, ones_mean)
        full_attention(nc, d, XR, ident, ones, ones_mean, q_parts, k_parts, v_rows)
        local_transformer(nc, d, XR, ident, ones, ones_mean)
        multi_query_attention(nc, d, XR, ident, ones, ones_mean, q_parts, k_parts, v_rows)
        fp4_mlp(nc, d, XR, ident, ones, ones_mean)
        store_residual(nc, out_t, XR)


def full_attention(nc, d, XR, ident, ones, ones_mean, q_parts, k_parts, v_rows):
    w = {"Wqkv_t": d["a0_wqkv_t"], "bqkv": d["a0_bqkv"], "bv_row": d["a0_bv_row"], "head_mean": d["c_head_mean"],
         "wq": d["a0_wq"], "wk": d["a0_wk"], "wo_pad": d["a0_wo_pad"], "bo": d["a0_bo"], "spread_den": d["c_spread_den"]}
    project_heads(nc, "proj0", XR, ident, ones, ones_mean, w, q_parts, k_parts, v_rows)
    attend(nc, "att0", XR, ident, w, q_parts, k_parts, v_rows, causal=False, many_keys=True)


def multi_query_attention(nc, d, XR, ident, ones, ones_mean, q_parts, k_parts, v_rows):
    w = {"w_down": d["a1_w_down"], "w_q": d["a1_w_q"], "w_kv": d["a1_w_kv"], "wo_pad": d["a1_wo_pad"],
         "causal": d["c_causal"], "spread_den": d["c_spread_den"]}
    project_heads(nc, "proj1", XR, ident, ones, ones_mean, w, q_parts, k_parts[:, 0:HD, :], v_rows[:, 0:HD])
    attend(nc, "att1", XR, ident, w, q_parts, k_parts[:, 0:HD, :], v_rows[:, 0:HD], causal=True, many_keys=False)


def layout(inputs):
    f = {k: np.asarray(v) for k, v in inputs.items()}
    a = {"x_t": f["L0_attn_x"].reshape(TOK, P).T}
    a["a0_wqkv_t"] = f["L0_attn_Wqkv"].T
    a["a0_bqkv"] = f["L0_attn_bqkv"].reshape(3 * P, 1)
    a["a0_bv_row"] = f["L0_attn_bqkv"][2 * P:].reshape(1, P)
    a["a0_wq"] = np.tile(f["L0_attn_wq"], HEADS).reshape(P, 1)
    a["a0_wk"] = np.tile(f["L0_attn_wk"], HEADS).reshape(P, 1)
    a["a0_wo_pad"] = pad_heads(f["L0_attn_Wo"].T)
    a["a0_bo"] = f["L0_attn_bo"].reshape(P, 1)
    a["a1_w_down"] = f["L1_attn_Wc_down"]
    a["a1_w_q"] = f["L1_attn_Wq_up"]
    a["a1_w_kv"] = f["L1_attn_Wkv_up"]
    a["a1_wo_pad"] = pad_heads(f["L1_attn_Wc_proj"])
    a.update(layout_more(f))
    a.update(layout_fp4(f))
    a.update(host_constants())
    return {k: np.ascontiguousarray(v) for k, v in a.items()}


def kernel(**inputs):
    import concourse.bacc as bacc
    from concourse.bass_utils import run_bass_kernel_spmd

    nc = bacc.Bacc("TRN2", target_bir_lowering=False, num_devices=1)
    arrays = layout(inputs)
    dram = {n: nc.dram_tensor(n, a.shape, mybir.dt.from_np(a.dtype), kind="ExternalInput").ap() for n, a in arrays.items()}
    out_t = nc.dram_tensor("out_t", (P, TOK), F32, kind="ExternalOutput").ap()
    build(nc, dram, out_t)
    r = run_bass_kernel_spmd(nc, [arrays], core_ids=[0])
    return np.ascontiguousarray(r.results[0]["out_t"].T).reshape(BATCH, SEQ, P)
```
